# Optimizing a Trainium2 kernel written in Bass

```python
import numpy as np
import jax
import jax.numpy as jnp

def _softmax(x, axis=-1):
    return jax.nn.softmax(x, axis=axis)

def _gelu(x):
    return jax.nn.gelu(x, approximate=True)

def _silu(x):
    return jax.nn.silu(x)

def _sigmoid(x):
    return jax.nn.sigmoid(x)

def _layernorm(x, axis=-1, eps=1e-05):
    m = jnp.mean(x, axis=axis, keepdims=True)
    v = jnp.var(x, axis=axis, keepdims=True)
    return (x - m) / jnp.sqrt(v + eps)

def _scatter_add(tgt, idx, src, axis=0):
    return tgt.at[idx].add(src)

def _segment_sum(src, seg, n):
    return jax.ops.segment_sum(src, seg, n)
kernel_name = 'mk_adj_preln_d1_adj_r2_1c4a02'

def setup_inputs(seed: int=0):
    np.random.seed(seed)
    _w = jnp.asarray

    def _rec_inputs():
        import jax
        import jax.numpy as jnp
        _gk = jax.random.key(seed)
        x = 7.22e-05 + 1 * jax.random.normal(jax.random.fold_in(_gk, 1), (16, 512, 512), jnp.float32)
        _a = jax.random.bernoulli(jax.random.fold_in(_gk, 2), 0.03125, (16, 512, 512))
        _a = jnp.logical_or(_a, jnp.swapaxes(_a, -1, -2))
        _a = jnp.logical_or(_a, jnp.eye(512, dtype=bool))
        _af = _a.astype(jnp.float32)
        _af = _af * jax.random.uniform(jax.random.fold_in(_gk, 3), (16, 512, 512), jnp.float32, 0.05, 4.42607)
        adj = _af
        return (x, adj)
    x, adj = _rec_inputs()

    def _L0_gnn_setup():
        import jax, jax.numpy as jnp
        import numpy as np
        NUM_HEADS = 16
        key = jax.random.key(seed)
        ks = jax.random.split(key, 7)
        B, N, D = (16, 256, 512)
        return {'x': jax.random.normal(ks[0], (B, N, D), dtype=jnp.float32), 'spatial_encoding': jax.random.normal(ks[1], (B, N, N), dtype=jnp.float32), 'edge_encoding': jax.random.normal(ks[2], (B, N, N), dtype=jnp.float32), 'Wq': jax.random.normal(ks[3], (D, D), dtype=jnp.float32) * D ** (-0.5), 'Wk': jax.random.normal(ks[4], (D, D), dtype=jnp.float32) * D ** (-0.5), 'Wv': jax.random.normal(ks[5], (D, D), dtype=jnp.float32) * D ** (-0.5), 'Wo': jax.random.normal(ks[6], (D, D), dtype=jnp.float32) * D ** (-0.5)}
    _L0_gnn_all = _L0_gnn_setup()
    _L0_gnn_in = {k: v for k, v in _L0_gnn_all.items() if k in ('Wq', 'Wk', 'Wv', 'Wo')}
    del _L0_gnn_all
    return {'x': x, 'adj': adj, 'L0_gnn_Wq': _L0_gnn_in['Wq'], 'L0_gnn_Wk': _L0_gnn_in['Wk'], 'L0_gnn_Wv': _L0_gnn_in['Wv'], 'L0_gnn_Wo': _L0_gnn_in['Wo']}

def reference(x, adj, L0_gnn_Wq, L0_gnn_Wk, L0_gnn_Wv, L0_gnn_Wo):
    import jax
    import jax.numpy as jnp

    def _L0_gnn_ref(x, spatial_encoding, edge_encoding, Wq, Wk, Wv, Wo):
        import jax, jax.numpy as jnp
        import numpy as np
        NUM_HEADS = 16
        B, N, D = x.shape
        H = NUM_HEADS
        hd = D // H
        scale = D ** (-0.5)

        def split_heads(t):
            return t.reshape(B, N, H, hd).transpose(0, 2, 1, 3)
        q = split_heads(x @ Wq.T)
        k = split_heads(x @ Wk.T)
        v = split_heads(x @ Wv.T)
        bias = (spatial_encoding + edge_encoding)[:, None]
        a = jnp.einsum('bhnd,bhmd->bhnm', q, k) * scale + bias
        row_nonzero = jnp.any(a != 0, axis=-1, keepdims=True)
        a = jnp.where(row_nonzero, a, -jnp.inf)
        p = jax.nn.softmax(a, axis=-1)
        p = jnp.where(jnp.isnan(p), 0.0, p)
        o = jnp.einsum('bhnm,bhmd->bhnd', p, v)
        o = o.transpose(0, 2, 1, 3).reshape(B, N, D)
        return o @ Wo.T
    h = jnp.maximum(_layernorm(x, axis=-1), 0.0)
    x = x + _L0_gnn_ref(h, adj, adj, L0_gnn_Wq, L0_gnn_Wk, L0_gnn_Wv, L0_gnn_Wo)
    return x

_drawn_inputs = setup_inputs


def setup_inputs(seed=0):
    import zlib

    import numpy as np

    out = dict(_drawn_inputs(seed))
    spreads = {}
    factors = {'L0_gnn_Wq': 3.249, 'L0_gnn_Wk': 3.203}
    for name, (base, spread) in spreads.items():
        noise = np.random.default_rng([zlib.crc32(name.encode()), seed]).standard_normal(out[name].shape)
        drawn = base * np.exp(spread * noise) if base else spread * noise
        out[name] = jnp.asarray(drawn.astype(out[name].dtype))
    for name, factor in factors.items():
        out[name] = (out[name] * factor).astype(out[name].dtype)
    return out
```

```python
from contextlib import ExitStack

import concourse.bass as bass
from concourse import mybir

ALU = mybir.AluOpType
ACT = mybir.ActivationFunctionType
F32 = mybir.dt.float32
F32R = mybir.dt.float32r

P = 128
HEADS = 16
EPS = 1e-5
LAG = 3
RING = 4
GROUPS_PER_CHUNK = 4


def graph_attention(nc, x, adj, wq_t, wk_t, wv_t, wo_t, out):
    B, N, D = x.shape
    HD = D // HEADS
    NT = N // P
    KT = D // P
    PER = P // HD
    CHUNKS = HEADS // PER
    UNITS = HEADS * NT
    CU = UNITS // CHUNKS
    GROUPS = UNITS // PER
    SCALE = float(D) ** -0.5
    STACK_DMAS = 3 * PER
    assert (N, D, HD, NT, KT, PER, CHUNKS, CU) == (512, 512, 32, 4, 4, 4, 4, 16)

    with ExitStack() as ctx:
        def sb(name, shape, dt=F32):
            return ctx.enter_context(nc.sbuf_tensor(name, shape, dt))

        def ps(name, shape):
            return ctx.enter_context(nc.psum_tensor(name, shape, F32))

        def sem(name):
            return ctx.enter_context(nc.semaphore(name))

        w_hi = {k: sb(f"w{k}_hi", [P, KT, D], F32R) for k in "qkvo"}
        w_lo = {k: sb(f"w{k}_lo", [P, KT, D], F32R) for k in "qkvo"}
        qk_stack = [sb(f"qk_stack{i}", [3 * HD, 2, PER, N], F32R) for i in range(2)]
        q_stack = [stack[:, 0] for stack in qk_stack]
        k_stack = [stack[:, 1] for stack in qk_stack]
        qk_parts = sb("qk_parts", [P, 4, N], F32R)
        q_lo, q_hi, k_hi, k_lo = (qk_parts[:, i, :] for i in range(4))
        hT_hi = sb("hT_hi", [P, KT, N], F32R)
        hT_lo = sb("hT_lo", [P, KT, N], F32R)
        x_sb = sb("x_sb", [P, NT, D])
        adj_sb = sb("adj_sb", [P, NT, N])
        bias = sb("bias", [P, NT, N])
        v_sb = sb("v_sb", [P, NT, D])
        v_side = sb("v_side", [P, NT, P])
        ring = sb("ring", [P, RING, N])
        pT = sb("pT", [P, 2, PER, N])
        oT = sb("oT", [P, N])
        oT_hi = sb("oT_hi", [P, CHUNKS, N], F32R)
        oT_lo = sb("oT_lo", [P, CHUNKS, N], F32R)
        out_sb = sb("out_sb", [P, NT, D])
        ident = sb("ident", [P, P])
        stats = sb("stats", [P, NT, 6])
        mean_var = sb("mean_var", [P, NT, 2])
        var_eps = sb("var_eps", [P, NT])
        rstd = sb("rstd", [P, NT])
        consts = sb("consts", [P, 2, NT])
        neg_max = sb("neg_max", [P, UNITS])
        row_sum = sb("row_sum", [P, UNITS])
        r_small = sb("r_small", [P, 4, CU])
        r_row = sb("r_row", [P, CU, HD])
        stage = pT

        s_ps = ps("s_ps", [P, 2, N])
        t_ps = ps("t_ps", [P, 2, N])
        o_ps = ps("o_ps", [P, N])
        proj_ps = ps("proj_ps", [P, 2, N])
        misc_ps = ps("misc_ps", [P, N])

        ident_ready = sem("ident_ready")
        consts_ready = sem("consts_ready")
        w_in = [sem(f"w_in{i}") for i in range(2)]
        w_hi_done = sem("w_hi_done")
        w_lo_done = sem("w_lo_done")
        x_in = sem("x_in")
        adj_in = sem("adj_in")
        bias_done = sem("bias_done")
        stats_done = sem("stats_done")
        aggr_done = sem("aggr_done")
        rstd_done = sem("rstd_done")
        h_done = sem("h_done")
        hT_made = sem("hT_made")
        hT_hi_done = sem("hT_hi_done")
        hT_lo_done = sem("hT_lo_done")
        q_made = sem("q_made")
        k_made = sem("k_made")
        q_hi_done = sem("q_hi_done")
        k_hi_done = sem("k_hi_done")
        q_lo_done = sem("q_lo_done")
        k_lo_done = sem("k_lo_done")
        stack_in = sem("stack_in")
        v_made = sem("v_made")
        v_copied = sem("v_copied")
        v_moved = sem("v_moved")
        scores = sem("scores")
        neg_a = sem("neg_a")
        probs = sem("probs")
        probs_T = sem("probs_T")
        pT_copied = sem("pT_copied")
        pv = sem("pv")
        r_step = sem("r_step")
        r_done = sem("r_done")
        r_T = sem("r_T")
        r_copied = sem("r_copied")
        oT_done = sem("oT_done")
        oT_hi_done = sem("oT_hi_done")
        oT_lo_done = sem("oT_lo_done")
        o_made = sem("o_made")
        out_done = sem("out_done")
        resid_in = sem("resid_in")
        stored = sem("stored")

        x_t = x.rearrange("b (t p) d -> b p t d", p=P)
        adj_t = adj.rearrange("b (t p) m -> b p t m", p=P)
        out_t = out.rearrange("b (t p) d -> b p t d", p=P)

        def f(ap):
            return ap.bitcast(F32)

        def unit(u):
            c, rest = divmod(u % UNITS, CU)
            nt, j = divmod(rest, PER)
            return c, nt, j

        def samples(eng, body, peeled=1):
            body(0, first=True)
            for b in range(1, peeled):
                body(b)
            with eng.Fori(peeled, B - 1) as b:
                body(b)
            body(B - 1, last=True)
            body(B, drain=True)

        block = ctx.enter_context(nc.Block())

        @block.sync
        def _(sp):
            for n, (k, w) in enumerate((("q", wq_t), ("k", wk_t), ("v", wv_t), ("o", wo_t))):
                if n >= 2:
                    sp.wait_ge(w_lo_done, n - 1)
                sp.dma_start(stage[:, n % 2], w.rearrange("(t p) n -> p t n", p=P)).then_inc(w_in[n % 2], 16)

            def load_x(b):
                sp.dma_start(x_sb[:, :, :], x_t[b]).then_inc(x_in, 16)

            def load_adj(b):
                sp.dma_start(adj_sb[:, :, :], adj_t[b]).then_inc(adj_in, 16)

            def fill_stack(b, c):
                n = b * CHUNKS + (c + 1)
                sp.wait_ge(q_lo_done, n)
                sp.wait_ge(k_lo_done, n)
                for row, parts in enumerate((slice(1, 3), slice(0, 3, 2), slice(1, 4, 2))):
                    for j in range(PER):
                        sp.dma_start(f(qk_stack[c % 2][row * HD:(row + 1) * HD, :, j, :]),
                                     f(qk_parts[j * HD:(j + 1) * HD, parts, :])).then_inc(stack_in, 16)

            def body(b, first=False, last=False, drain=False):
                if not last and not drain:
                    sp.wait_ge(hT_made, b * KT + KT)
                    load_x(b + 1)
                    sp.wait_ge(bias_done, b + 1)
                    load_adj(b + 1)
                if not first:
                    if not (isinstance(b, int) and b == 1):
                        sp.wait_ge(stored, b * (16 * NT) - 16 * NT)
                    sp.dma_start(out_sb[:, :, :], x_t[b - 1]).then_inc(resid_in, 16)
                if not drain:
                    fill_stack(b, 1)
                if not first:
                    for nt in range(NT):
                        sp.wait_ge(out_done, b * NT + (nt + 1 - NT))
                        sp.dma_start(out_t[b - 1][:, nt, :], out_sb[:, nt, :]).then_inc(stored, 16)
                if not drain:
                    fill_stack(b, 2)
                    fill_stack(b, 3)
                if not last and not drain:
                    fill_stack(b + 1, 0)

            load_x(0)
            load_adj(0)
            fill_stack(0, 0)
            samples(sp, body, peeled=2)
            sp.wait_ge(stored, B * NT * 16)

        @block.tensor
        def _(pe):
            def split_product(out_ps, pairs, part, parts):
                steps = [(l, r) for lhs, rhs in pairs for l, r in ((lhs[0], rhs[0]), (lhs[1], rhs[0]), (lhs[0], rhs[1]))]
                share = len(steps) // parts
                for i in range(part * share, (part + 1) * share):
                    mm = nc.tensor.matmul(out_ps, steps[i][0], steps[i][1], start=(i == 0), stop=(i == len(steps) - 1))
                return mm if part == parts - 1 else None

            def qk(b, c, which, part):
                bank = "qk".index(which)
                if part == 0:
                    pe.wait_ge(hT_lo_done, b * KT + KT)
                    pe.wait_ge((q_lo_done, k_lo_done)[bank], b * CHUNKS + c)
                    if c == 1:
                        pe.wait_ge(v_copied, (b + 1) * 2 * NT)
                    if c == 2 and not (isinstance(b, int) and b == 0):
                        pe.wait_ge(out_done, b * NT + (bank - 1))
                cols = slice(c * P, (c + 1) * P)
                mm = split_product(proj_ps[:, bank, :],
                                   [((w_hi[which][:, k, cols], w_lo[which][:, k, cols]), (hT_hi[:, k, :], hT_lo[:, k, :]))
                                    for k in range(KT)], part, 4)
                if mm:
                    mm.then_inc((q_made, k_made)[bank], 1)

            def v_rows(b, nt, part):
                if part == 0:
                    if nt < 2:
                        pe.wait_ge((q_lo_done, k_lo_done)[nt], b * CHUNKS + 1)
                    else:
                        pe.wait_ge(v_copied, b * (2 * NT) + 2 * (nt - 1))
                rows = slice(nt * P, (nt + 1) * P)
                mm = split_product(proj_ps[:, nt % 2, :],
                                   [((hT_hi[:, k, rows], hT_lo[:, k, rows]), (w_hi["v"][:, k, :], w_lo["v"][:, k, :]))
                                    for k in range(KT)], part, 2)
                if mm:
                    mm.then_inc(v_made, 1)

            def o_rows(b, nt, part):
                if part == 0:
                    if nt == 0:
                        pe.wait_ge(oT_lo_done, b * CHUNKS + CHUNKS)
                    if nt < 2:
                        if not (isinstance(b, int) and b == B - 1):
                            pe.wait_ge((q_lo_done, k_lo_done)[nt], b * CHUNKS + (CHUNKS + 2))
                    else:
                        pe.wait_ge(out_done, b * NT + (nt - 1))
                rows = slice(nt * P, (nt + 1) * P)
                mm = split_product(proj_ps[:, nt % 2, :],
                                   [((oT_hi[:, k, rows], oT_lo[:, k, rows]), (w_hi["o"][:, k, :], w_lo["o"][:, k, :]))
                                    for k in range(KT)], part, 2)
                if mm:
                    mm.then_inc(o_made, 1)

            def transpose_h(b, k):
                if k == 0:
                    pe.wait_ge(h_done, b * NT + NT)
                    if not (isinstance(b, int) and b == 0):
                        pe.wait_ge(r_copied, b * CHUNKS - 2)
                else:
                    pe.wait_ge(hT_lo_done, b * KT + k)
                for nt in range(NT):
                    mm = nc.tensor.transpose(misc_ps[:, nt * P:(nt + 1) * P], x_sb[:, nt, k * P:(k + 1) * P], ident[:, :])
                mm.then_inc(hT_made, 1)

            def make_scores(b, u):
                c, nt, j = unit(u)
                if u % CU == 0:
                    pe.wait_ge(stack_in, b * (CHUNKS * STACK_DMAS * 16) + (c + 1) * STACK_DMAS * 16)
                if not (isinstance(b, int) and b * UNITS + u < 2):
                    pe.wait_ge(neg_a, b * UNITS + (u - 1))
                nc.tensor.matmul(s_ps[:, u % 2, :], q_stack[c % 2][:, j, nt * P:(nt + 1) * P], k_stack[c % 2][:, j, :],
                                 start=True, stop=True).then_inc(scores, 1)

            def transpose_probs(b, u):
                pe.wait_ge(probs, b * UNITS + (u + 1))
                if not (isinstance(b, int) and b * UNITS + u < 2):
                    pe.wait_ge(pT_copied, b * UNITS + (u - 1))
                for m in range(NT):
                    mm = nc.tensor.transpose(t_ps[:, u % 2, m * P:(m + 1) * P], ring[:, u % RING, m * P:(m + 1) * P],
                                             ident[:, :])
                mm.then_inc(probs_T, 1)

            def spread_r(b, c):
                pe.wait_ge(r_done, b * CHUNKS + (c + 1))
                pe.wait_ge(hT_lo_done, b * KT + (KT if c < 2 else 2 * KT) if not isinstance(b, int) or b < B - 1 or c < 2
                           else B * KT)
                if not (isinstance(b, int) and b == 0 and c == 0):
                    pe.wait_ge(r_copied, b * CHUNKS + c)
                for nt in range(NT):
                    mm = nc.tensor.transpose(misc_ps[:, nt * P:(nt + 1) * P],
                                             r_row[:, nt * PER:(nt + 1) * PER, :].rearrange("p j d -> p (j d)"),
                                             ident[:, :])
                mm.then_inc(r_T, 1)

            def weigh_v(b, g):
                c, nt = divmod(g % GROUPS, NT)
                pe.wait_ge(pT_copied, b * UNITS + (g + 1) * PER)
                if nt == 0 and not (isinstance(b, int) and b == 0 and g == 0):
                    pe.wait_ge(oT_done, b * CHUNKS + c if g >= 0 else b * CHUNKS - 1)
                if c == CHUNKS - 1 and nt == 0:
                    pe.wait_ge(v_moved, b + 1)
                for m in range(NT):
                    for j in range(PER):
                        h = c * PER + j
                        mm = nc.tensor.matmul(o_ps[j * HD:(j + 1) * HD, nt * P:(nt + 1) * P],
                                              v_sb[:, m, h * HD:(h + 1) * HD], pT[:, g % 2, j, m * P:(m + 1) * P],
                                              start=(m == 0), stop=(m == NT - 1), skip_group_check=True)
                mm.then_inc(pv, 1)

            def body(b, first=False, last=False, drain=False):
                for u in range(UNITS if not drain else CU):
                    c, t = divmod(u, CU)
                    if not drain:
                        make_scores(b, u)
                    if t < 8 and not drain and not (last and c == CHUNKS - 1):
                        nb, ncx = (b, c + 1) if c < CHUNKS - 1 else (b + 1, 0)
                        qk(nb, ncx, "qk"[t // 4], t % 4)
                    if t >= 8 and c == 0 and not first:
                        o_rows(b - 1, (t - 8) // 2, t % 2)
                    if t >= 8 and t % 2 == 0 and c == 2 and not last:
                        transpose_h(b + 1, (t - 8) // 2)
                    if t >= 8 and c == 3 and not last:
                        v_rows(b + 1, (t - 8) // 2, t % 2)
                    if not (first and u < LAG) and not (drain and u >= LAG):
                        transpose_probs(b, u - LAG)
                    if t == 4 and not (first and c == 0):
                        spread_r(b if c else b - 1, (c - 1) % CHUNKS)
                    if u % PER == 3 and not (first and u < 7) and not (drain and u > 3):
                        weigh_v(b, (u - 7) // PER)

            pe.wait_ge(ident_ready, 2)
            for k in range(KT):
                transpose_h(0, k)
            pe.wait_ge(w_lo_done, 4)
            for which in "qk":
                for part in range(4):
                    if part == 0:
                        if which == "q":
                            pe.wait_ge(hT_lo_done, KT)
                    mm = split_product(proj_ps[:, "qk".index(which), :],
                                       [((w_hi[which][:, k, 0:P], w_lo[which][:, k, 0:P]), (hT_hi[:, k, :], hT_lo[:, k, :]))
                                        for k in range(KT)], part, 4)
                mm.then_inc(q_made if which == "q" else k_made, 1)
            for nt in range(NT):
                for part in range(2):
                    v_rows(0, nt, part)
            samples(pe, body)

        @block.vector
        def _(dve):
            for n, k in enumerate("qkvo"):
                dve.wait_ge(w_hi_done, n + 1)
                nc.vector.tensor_tensor(w_lo[k][:, :, :], stage[:, n % 2], f(w_hi[k][:, :, :]),
                                        ALU.subtract).then_inc(w_lo_done, 1)

            def copy_pT(b, u):
                c, nt, j = unit(u)
                g = u // PER
                dve.wait_ge(probs_T, b * UNITS + (u + 1))
                if j == 0 and not (isinstance(b, int) and b * GROUPS + g < 2):
                    dve.wait_ge(pv, b * GROUPS + (g - 1))
                nc.vector.tensor_copy(pT[:, g % 2, j, :], t_ps[:, u % 2, :]).then_inc(pT_copied, 1)

            def add_bias_and_max(b, u, wait):
                if wait:
                    dve.wait_ge(scores, b * UNITS + (u + 1))
                nc.vector.tensor_tensor_reduce(ring[:, u % RING, :], s_ps[:, u % 2, :], bias[:, unit(u)[1], :], 1.0, 3e38,
                                               ALU.add, ALU.min, neg_max[:, u:u + 1]).then_inc(neg_a, 1)

            def make_bias(b):
                dve.wait_ge(adj_in, b * 16 + 16)
                if not (isinstance(b, int) and b == 0):
                    dve.wait_ge(neg_a, b * UNITS)
                nc.vector.tensor_scalar(bias[:, :, :], adj_sb[:, :, :], -2.0, None, ALU.mult).then_inc(bias_done, 1)
                dve.wait_ge(bias_done, b + 1)

            def row_stats(b, nt):
                if nt == 0:
                    dve.wait_ge(x_in, b * 16 + 16)
                nc.vector.bn_stats(stats[:, nt, :], x_sb[:, nt, :]).then_inc(stats_done, 1)

            def aggregate(b):
                if isinstance(b, int):
                    dve.wait_ge(stats_done, b * NT + NT)
                for nt in range(NT):
                    nc.vector.bn_aggr(mean_var[:, nt, :], stats[:, nt, :]).then_inc(aggr_done, 1)

            def normalise(b, nt):
                dve.wait_ge(rstd_done, b * 2 + 2)
                nc.vector.tensor_scalar(x_sb[:, nt, :], x_sb[:, nt, :], mean_var[:, nt, 0:1], rstd[:, nt:nt + 1],
                                        ALU.subtract, ALU.mult).then_inc(h_done, 1)

            def split_hT(b, k):
                dve.wait_ge(hT_hi_done, b * KT + (k + 1))
                nc.vector.scalar_tensor_tensor(out=hT_lo[:, k, :], in0=misc_ps[:, :], scalar=0.0, in1=f(hT_hi[:, k, :]),
                                               op0=ALU.max, op1=ALU.subtract).then_inc(hT_lo_done, 1)

            def split_q(b, c):
                dve.wait_ge(q_hi_done, b * CHUNKS + (c + 1))
                nc.vector.scalar_tensor_tensor(out=q_lo, in0=proj_ps[:, 0, :], scalar=-SCALE, in1=f(q_hi),
                                               op0=ALU.mult, op1=ALU.subtract).then_inc(q_lo_done, 1)

            def split_k(b, c):
                dve.wait_ge(k_hi_done, b * CHUNKS + (c + 1))
                nc.vector.tensor_tensor(k_lo, proj_ps[:, 1, :], f(k_hi), ALU.subtract).then_inc(k_lo_done, 1)

            def invert_sums(b, c):
                cols = slice(c * CU, (c + 1) * CU)
                n = b * (4 * CHUNKS) + 4 * c
                dve.wait_ge(probs, b * UNITS + (c + 1) * CU)
                if not (isinstance(b, int) and b == 0 and c == 0):
                    dve.wait_ge(r_done, b * CHUNKS + c)
                nc.vector.reciprocal(r_small[:, 0, :], row_sum[:, cols]).then_inc(r_step, 1)
                nc.vector.tensor_scalar(r_small[:, 1, :], neg_max[:, cols], 0.0, None, ALU.is_equal).then_inc(r_step, 1)
                dve.wait_ge(r_step, n + 2)
                nc.vector.scalar_tensor_tensor(out=r_small[:, 2, :], in0=row_sum[:, cols], scalar=float(N),
                                               in1=r_small[:, 1, :], op0=ALU.is_equal, op1=ALU.mult).then_inc(r_step, 1)
                dve.wait_ge(r_step, n + 3)
                nc.vector.tensor_scalar(r_small[:, 3, :], r_small[:, 2, :], 0.0, None, ALU.is_equal).then_inc(r_step, 1)

            def normalise_o(b, c):
                dve.wait_ge(r_copied, b * CHUNKS + (c + 1))
                dve.wait_ge(pv, b * GROUPS + (c + 1) * NT)
                nc.vector.tensor_tensor(oT[:, :], o_ps[:, :], oT[:, :], ALU.mult).then_inc(oT_done, 1)

            def move_v(b):
                dve.wait_ge(v_copied, (b + 1) * (2 * NT))
                if not (isinstance(b, int) and b == 0):
                    dve.wait_ge(pv, b * GROUPS)
                nc.vector.tensor_copy(v_sb[:, :, (CHUNKS - 1) * P:D], v_side[:, :, :]).then_inc(v_moved, 1)

            def add_residual(b, nt):
                if nt == 0:
                    dve.wait_ge(resid_in, b * 16 + 16)
                dve.wait_ge(o_made, b * NT + (nt + 1))
                nc.vector.tensor_tensor(out_sb[:, nt, :], proj_ps[:, nt % 2, :], out_sb[:, nt, :],
                                        ALU.add).then_inc(out_done, 1)

            def body(b, first=False, last=False, drain=False):
                for u in range(UNITS if not drain else CU + 1):
                    c, t = divmod(u, CU)
                    transposed = not (first and u < LAG) and not (drain and u >= LAG)
                    if c == 1 and t == 13 and not last and not drain:
                        dve.wait_ge(stats_done, b * NT + 2 * NT)
                    if transposed:
                        copy_pT(b, u - LAG)
                    if not drain:
                        add_bias_and_max(b, u, not transposed)
                    if t == 2 and not (first and c == 0) and not (drain and c):
                        invert_sums(b if c else b - 1, (c - 1) % CHUNKS)
                    if t == 5 and not (first and c == 0):
                        normalise_o(b if c else b - 1, (c - 1) % CHUNKS)
                    if t in (5, 8) and not drain and not (last and c == CHUNKS - 1):
                        nb, ncx = (b, c + 1) if c < CHUNKS - 1 else (b + 1, 0)
                        (split_q if t == 5 else split_k)(nb, ncx)
                    if c == 0 and t == 6 and not drain:
                        move_v(b)
                    if not first and u in (10, 12, 14, 16):
                        add_residual(b - 1, (u - 10) // 2)
                    if not last and not drain:
                        if c == 1 and t in (3, 6, 9, 11):
                            row_stats(b + 1, (3, 6, 9, 11).index(t))
                        if c == 1 and t == 13:
                            aggregate(b + 1)
                        if c == 2 and t in (0, 1, 3, 6):
                            normalise(b + 1, (0, 1, 3, 6).index(t))
                        if c == 2 and t in (9, 11, 13, 15):
                            split_hT(b + 1, (t - 9) // 2)
                if not last and not drain:
                    make_bias(b + 1)

            for nt in range(NT):
                row_stats(0, nt)
            aggregate(0)
            for nt in range(NT):
                normalise(0, nt)
            make_bias(0)
            for k in range(KT):
                split_hT(0, k)
            split_q(0, 0)
            split_k(0, 0)
            samples(dve, body)

        @block.scalar
        def _(act):
            for n, k in enumerate("qkvo"):
                act.wait_ge(w_in[n % 2], 16 * (n // 2 + 1))
                nc.scalar.activation(w_hi[k][:, :, :], stage[:, n % 2], ACT.Copy).then_inc(w_hi_done, 1)

            def exponentials(b, u):
                act.wait_ge(neg_a, b * UNITS + (u + 1))
                nc.scalar.activation(ring[:, u % RING, :], ring[:, u % RING, :], ACT.Exp, bias=neg_max[:, u:u + 1],
                                     scale=-1.0, accum_out=row_sum[:, u:u + 1]).then_inc(probs, 1)

            def round_hT(b, k):
                act.wait_ge(hT_made, b * KT + (k + 1))
                if k == 0 and not (isinstance(b, int) and b == 0):
                    act.wait_ge(k_made, b * CHUNKS)
                nc.scalar.activation(hT_hi[:, k, :], misc_ps[:, :], ACT.Relu).then_inc(hT_hi_done, 1)

            def round_q(b, c):
                act.wait_ge(q_made, b * CHUNKS + (c + 1))
                if not (isinstance(b, int) and b == 0 and c == 0):
                    act.wait_ge(stack_in, b * (CHUNKS * STACK_DMAS * 16) + c * STACK_DMAS * 16)
                nc.scalar.activation(q_hi, proj_ps[:, 0, :], ACT.Copy, scale=-SCALE).then_inc(q_hi_done, 1)

            def round_k(b, c):
                act.wait_ge(k_made, b * CHUNKS + (c + 1))
                nc.scalar.activation(k_hi, proj_ps[:, 1, :], ACT.Copy).then_inc(k_hi_done, 1)

            def copy_v(b, nt):
                act.wait_ge(v_made, b * NT + (nt + 1))
                if nt == 0 and not (isinstance(b, int) and b == 0):
                    act.wait_ge(pv, b * GROUPS - NT)
                    act.wait_ge(v_moved, b)
                cut = (CHUNKS - 1) * P
                nc.scalar.activation(v_sb[:, nt, 0:cut], proj_ps[:, nt % 2, 0:cut], ACT.Copy).then_inc(v_copied, 1)
                nc.scalar.activation(v_side[:, nt, :], proj_ps[:, nt % 2, cut:D], ACT.Copy).then_inc(v_copied, 1)

            def copy_r(b, c):
                act.wait_ge(r_T, b * CHUNKS + (c + 1))
                if not (isinstance(b, int) and b == 0 and c == 0):
                    act.wait_ge(oT_lo_done, b * CHUNKS + c)
                nc.scalar.activation(oT[:, :], misc_ps[:, :], ACT.Copy).then_inc(r_copied, 1)

            def round_o(b, c):
                act.wait_ge(oT_done, b * CHUNKS + (c + 1))
                if c == 0 and not (isinstance(b, int) and b == 0):
                    act.wait_ge(o_made, b * NT)
                nc.scalar.activation(oT_hi[:, c, :], oT[:, :], ACT.Copy).then_inc(oT_hi_done, 1)

            def body(b, first=False, last=False, drain=False):
                for u in range(UNITS if not drain else CU):
                    c, t = divmod(u, CU)
                    if not drain:
                        exponentials(b, u)
                    if t == 4 and not (first and c == 0):
                        copy_r(b if c else b - 1, (c - 1) % CHUNKS)
                    if t in (4, 7) and not drain and not (last and c == CHUNKS - 1):
                        nb, ncx = (b, c + 1) if c < CHUNKS - 1 else (b + 1, 0)
                        (round_q if t == 4 else round_k)(nb, ncx)
                    if t == 6 and not (first and c == 0):
                        round_o(b if c else b - 1, (c - 1) % CHUNKS)
                    if not last and not drain:
                        if c == 2 and t in (8, 10, 12, 14):
                            round_hT(b + 1, (t - 8) // 2)
                        if c == 3 and t in (9, 11, 13, 15):
                            copy_v(b + 1, (t - 9) // 2)

            for k in range(KT):
                round_hT(0, k)
            round_q(0, 0)
            round_k(0, 0)
            for nt in range(NT):
                copy_v(0, nt)
            samples(act, body)

        @block.gpsimd
        def _(pool):
            nc.gpsimd.memset(ident[:, :], 0.0).then_inc(ident_ready, 1)
            nc.gpsimd.memset(consts[:, 0, :], EPS).then_inc(consts_ready, 1)
            nc.gpsimd.memset(consts[:, 1, :], -0.5).then_inc(consts_ready, 1)
            pool.wait_ge(ident_ready, 1)
            nc.gpsimd.affine_select(out=ident[:, :], in_=ident[:, :], compare_op=ALU.not_equal, fill=1.0, base=0,
                                    pattern=[[-1, P]], channel_multiplier=1).then_inc(ident_ready, 1)

            def inverse_deviation(b):
                pool.wait_ge(aggr_done, b * NT + NT)
                nc.gpsimd.tensor_tensor(var_eps[:, :], mean_var[:, :, 1], consts[:, 0, :], ALU.add).then_inc(rstd_done, 1)
                pool.wait_ge(rstd_done, b * 2 + 1)
                nc.gpsimd.tensor_tensor(rstd[:, :], var_eps[:, :], consts[:, 1, :], ALU.pow).then_inc(rstd_done, 1)

            def repeat_r(b, c):
                pool.wait_ge(r_step, b * (4 * CHUNKS) + 4 * (c + 1))
                if not (isinstance(b, int) and b == 0 and c == 0):
                    pool.wait_ge(r_T, b * CHUNKS + c)
                nc.gpsimd.tensor_tensor(r_row[:, :, :], r_small[:, 0, :].unsqueeze(2).to_broadcast([P, CU, HD]),
                                        r_small[:, 3, :].unsqueeze(2).to_broadcast([P, CU, HD]),
                                        ALU.mult).then_inc(r_done, 1)

            def split_o(b, c):
                pool.wait_ge(oT_hi_done, b * CHUNKS + (c + 1))
                nc.gpsimd.tensor_tensor(oT_lo[:, c, :], oT[:, :], f(oT_hi[:, c, :]), ALU.subtract).then_inc(oT_lo_done, 1)

            def body(b, first=False, last=False, drain=False):
                for c in range(CHUNKS if not drain else 1):
                    if not (first and c == 0):
                        repeat_r(b if c else b - 1, (c - 1) % CHUNKS)
                        split_o(b if c else b - 1, (c - 1) % CHUNKS)
                    if c == 1 and not last and not drain:
                        inverse_deviation(b + 1)

            pool.wait_ge(consts_ready, 2)
            inverse_deviation(0)
            samples(pool, body)


_INS = ["x", "adj", "wq_t", "wk_t", "wv_t", "wo_t"]


def kernel(x, adj, L0_gnn_Wq, L0_gnn_Wk, L0_gnn_Wv, L0_gnn_Wo):
    import numpy as np
    import concourse.bacc as bacc
    from concourse import mybir as mb
    from concourse.bass_utils import run_bass_kernel_spmd

    given = dict(zip(_INS, (x, adj, *(np.asarray(w).T for w in (L0_gnn_Wq, L0_gnn_Wk, L0_gnn_Wv, L0_gnn_Wo)))))
    nc = bacc.Bacc("TRN2", target_bir_lowering=False, num_devices=1)
    arrays, args = {}, []
    for name in _INS:
        a = np.ascontiguousarray(given[name])
        arrays[f"in_{name}"] = a
        args.append(nc.dram_tensor(f"in_{name}", a.shape, mb.dt.from_np(a.dtype), kind="ExternalInput").ap())
    shape = tuple(np.asarray(x).shape)
    args.append(nc.dram_tensor("out_0", shape, mb.dt.from_np(np.dtype("float32")), kind="ExternalOutput").ap())
    graph_attention(nc, *args)
    r = run_bass_kernel_spmd(nc, [arrays], core_ids=[0])
    return r.results[0]["out_0"]
```

```python
from contextlib import ExitStack

import concourse.bass as bass
from concourse import mybir

ALU = mybir.AluOpType
ACT = mybir.ActivationFunctionType
F32 = mybir.dt.float32
F32R = mybir.dt.float32r

P = 128
HEADS = 16
EPS = 1e-5
LAG = 3
RING = 4

QK_PLAN = {(1, "q"): (0, 4, 3), (1, "k"): (4, 4, 7), (2, "q"): (14, 3, 17), (2, "k"): (17, 3, 19),
           (3, "q"): (27, 4, 31), (3, "k"): (31, 4, 34), (0, "q"): (43, 3, 45), (0, "k"): (46, 4, 49)}
O_PLAN = ((8, 3), (11, 3), (20, 3), (23, 3))
STATS_PLAN = (25, 28, 29, 30)
NORMALISE_PLAN = (33, 34, 35, 36)
HT_SLOT = 38
V_PLAN = ((50, 3), (53, 4), (57, 3), (60, 4))

def graph_attention(nc, x, adj, wq_t, wk_t, wv_t, wo_t, out):
    B, N, D = x.shape
    HD = D // HEADS
    NT = N // P
    KT = D // P
    PER = P // HD
    CHUNKS = HEADS // PER
    UNITS = HEADS * NT
    CU = UNITS // CHUNKS
    GROUPS = UNITS // PER
    PAIRS = GROUPS // 2
    HALF_SCALE = 0.5 * float(D) ** -0.5
    STACK_DMAS = 3 * PER
    assert (N, D, HD, NT, KT, PER, CHUNKS, CU) == (512, 512, 32, 4, 4, 4, 4, 16)

    with ExitStack() as ctx:
        def sb(name, shape, dt=F32):
            return ctx.enter_context(nc.sbuf_tensor(name, shape, dt))

        def ps(name, shape):
            return ctx.enter_context(nc.psum_tensor(name, shape, F32))

        def sem(name):
            return ctx.enter_context(nc.semaphore(name))

        w_hi = {k: sb(f"w{k}_hi", [P, KT, D], F32R) for k in "qkvo"}
        w_lo = {k: sb(f"w{k}_lo", [P, KT, D], F32R) for k in "qkvo"}
        qk_stack = [sb(f"qk_stack{i}", [3 * HD, 2, PER, N], F32R) for i in range(2)]
        q_stack = [stack[:, 0] for stack in qk_stack]
        k_stack = [stack[:, 1] for stack in qk_stack]
        qk_parts = sb("qk_parts", [P, 4, N], F32R)
        q_lo, q_hi, k_hi, k_lo = (qk_parts[:, i, :] for i in range(4))
        hT_hi = sb("hT_hi", [P, KT, N], F32R)
        hT_lo = sb("hT_lo", [P, KT, N], F32R)
        rows = sb("rows", [P, NT, D])
        adj_sb = sb("adj_sb", [P, NT, N])
        v_sb = sb("v_sb", [P, NT, D])
        v_side = sb("v_side", [P, NT, P])
        ring = sb("ring", [P, RING, N])
        pT = sb("pT", [P, 4, PER, N])
        oT = sb("oT", [P, N])
        oT_hi = sb("oT_hi", [P, CHUNKS, N], F32R)
        oT_lo = sb("oT_lo", [P, CHUNKS, N], F32R)
        ident = sb("ident", [P, P])
        stats = sb("stats", [P, NT, 6])
        mean_var = sb("mean_var", [P, NT, 2])
        var_eps = sb("var_eps", [P, NT])
        rstd = sb("rstd", [P, NT])
        shift = sb("shift", [P, NT])
        consts = sb("consts", [P, 3, NT])
        neg_max = sb("neg_max", [P, UNITS])
        row_sum = sb("row_sum", [P, UNITS])
        r_small = sb("r_small", [P, 4, CU])
        shared = sb("shared", [P, N])
        r_row = shared[:, :].rearrange("p (u d) -> p u d", d=HD)
        hT_full = shared
        stage = pT

        s_ps = ps("s_ps", [P, 2, N])
        t_ps = ps("t_ps", [P, 2, N])
        o_ps = ps("o_ps", [P, N])
        proj_ps = ps("proj_ps", [P, 2, N])
        r_ps = ps("r_ps", [P, N])

        ident_ready = sem("ident_ready")
        consts_ready = sem("consts_ready")
        w_in = [sem(f"w_in{i}") for i in range(4)]
        w_hi_done = sem("w_hi_done")
        w_lo_done = sem("w_lo_done")
        x_in = [sem(f"x_in{nt}") for nt in range(NT)]
        adj_in = [sem(f"adj_in{nt}") for nt in range(NT)]
        stats_done = sem("stats_done")
        aggr_done = sem("aggr_done")
        rstd_done = sem("rstd_done")
        h_done = sem("h_done")
        hT_made = sem("hT_made")
        hT_hi_done = sem("hT_hi_done")
        hT_full_done = sem("hT_full_done")
        hT_lo_done = sem("hT_lo_done")
        q_made = sem("q_made")
        k_made = sem("k_made")
        q_hi_done = sem("q_hi_done")
        k_hi_done = sem("k_hi_done")
        q_lo_done = sem("q_lo_done")
        k_lo_done = sem("k_lo_done")
        stack_in = sem("stack_in")
        v_made = sem("v_made")
        v_copied = sem("v_copied")
        v_moved = sem("v_moved")
        scores = sem("scores")
        neg_a = sem("neg_a")
        probs = sem("probs")
        probs_T = sem("probs_T")
        pT_copied = sem("pT_copied")
        pv = sem("pv")
        r_step = sem("r_step")
        r_done = sem("r_done")
        r_T = sem("r_T")
        r_copied = sem("r_copied")
        oT_done = sem("oT_done")
        oT_hi_done = sem("oT_hi_done")
        oT_lo_done = sem("oT_lo_done")
        o_made = sem("o_made")
        out_done = sem("out_done")
        resid_in = sem("resid_in")
        stored = [sem(f"stored{nt}") for nt in range(NT)]

        x_t = x.rearrange("b (t p) d -> b p t d", p=P)
        adj_t = adj.rearrange("b (t p) m -> b p t m", p=P)
        out_t = out.rearrange("b (t p) d -> b p t d", p=P)

        def f(ap):
            return ap.bitcast(F32)

        def unit(u):
            c, rest = divmod(u % UNITS, CU)
            nt, j = divmod(rest, PER)
            return c, nt, j

        def samples(eng, body):
            body(0, first=True)
            with eng.Fori(1, B - 1) as b:
                body(b)
            body(B - 1, last=True)
            body(B, drain=True)

        block = ctx.enter_context(nc.Block())

        @block.sync
        def _(sp):
            def load_x(b, nt):
                sp.dma_start(rows[:, nt, :], x_t[b][:, nt, :]).then_inc(x_in[nt], 16)

            def load_adj(b, nt):
                if not (isinstance(b, int) and b == 0):
                    sp.wait_ge(neg_a, b * UNITS + ((nt + 1) * PER - CU))
                sp.dma_start(adj_sb[:, nt, :], adj_t[b][:, nt, :]).then_inc(adj_in[nt], 16)

            def fill_stack(b, c):
                n = b * CHUNKS + (c + 1)
                sp.wait_ge(q_lo_done, n)
                sp.wait_ge(k_lo_done, n)
                for row, parts in enumerate((slice(1, 3), slice(0, 3, 2), slice(1, 4, 2))):
                    for j in range(PER):
                        sp.dma_start(f(qk_stack[c % 2][row * HD:(row + 1) * HD, :, j, :]),
                                     f(qk_parts[j * HD:(j + 1) * HD, parts, :])).then_inc(stack_in, 16)

            def body(b, first=False, last=False, drain=False):
                if not first:
                    if not drain:
                        sp.wait_ge(hT_made, b * KT + KT)
                    sp.dma_start(rows[:, :, :], x_t[b - 1]).then_inc(resid_in, 16)
                if not drain:
                    fill_stack(b, 1)
                for tiles in ((0, 1), (2, 3)):
                    if not first:
                        for nt in tiles:
                            sp.wait_ge(out_done, b * NT + (nt + 1 - NT))
                            sp.dma_start(out_t[b - 1][:, nt, :], rows[:, nt, :]).then_inc(stored[nt], 16)
                    if not last and not drain:
                        for nt in tiles:
                            if not first:
                                sp.wait_ge(stored[nt], b * 16)
                            elif nt == 0:
                                sp.wait_ge(hT_made, b * KT + KT)
                            load_x(b + 1, nt)
                    if not drain:
                        fill_stack(b, 2 + tiles[0] // 2)
                if not last and not drain:
                    fill_stack(b + 1, 0)
                    for nt in range(NT):
                        load_adj(b + 1, nt)

            for nt in range(NT):
                load_x(0, nt)
            for n, w in enumerate((wq_t, wk_t, wv_t, wo_t)):
                sp.dma_start(stage[:, n], w.rearrange("(t p) n -> p t n", p=P)).then_inc(w_in[n], 16)
            for nt in range(NT):
                load_adj(0, nt)
            fill_stack(0, 0)
            samples(sp, body)
            for nt in range(NT):
                sp.wait_ge(stored[nt], B * 16)

        @block.tensor
        def _(pe):
            def split_product(out_ps, pairs, part, parts, wait=None):
                steps = [(l, r) for lhs, rhs in pairs for l, r in ((lhs[0], rhs[0]), (lhs[1], rhs[0]), (lhs[0], rhs[1]))]
                assert len(steps) % parts == 0
                share = len(steps) // parts
                if wait:
                    done, base = wait
                    pe.wait_ge(done, base + (((part + 1) * share - 1) // 3 + 1))
                for i in range(part * share, (part + 1) * share):
                    mm = nc.tensor.matmul(out_ps, steps[i][0], steps[i][1], start=(i == 0), stop=(i == len(steps) - 1))
                return mm if part == parts - 1 else None

            def qk(b, c, which, part, parts):
                bank = "qk".index(which)
                if part == 0:
                    if c == 0:
                        pe.wait_ge(hT_full_done, b * KT + (KT - 1 + bank))
                    elif c == 1:
                        pe.wait_ge(v_copied, b * (2 * NT) + 2 * (NT - 1 + bank))
                    elif c > 1 and not (isinstance(b, int) and b == 0):
                        pe.wait_ge(out_done, b * NT + (2 * c - 7 + bank))
                    else:
                        pe.wait_ge((q_lo_done, k_lo_done)[bank], b * CHUNKS + c)
                cols = slice(c * P, (c + 1) * P)
                mm = split_product(proj_ps[:, bank, :],
                                   [((w_hi[which][:, k, cols], w_lo[which][:, k, cols]), (hT_hi[:, k, :], hT_lo[:, k, :]))
                                    for k in range(KT)], part, parts, (hT_lo_done, b * KT) if c == 0 else None)
                if mm:
                    mm.then_inc((q_made, k_made)[bank], 1)

            def v_rows(b, nt, part, parts):
                if part == 0:
                    if nt < 2:
                        pe.wait_ge((q_lo_done, k_lo_done)[nt], b * CHUNKS + 1)
                    else:
                        pe.wait_ge(v_copied, b * (2 * NT) + 2 * (nt - 1))
                rows = slice(nt * P, (nt + 1) * P)
                mm = split_product(proj_ps[:, nt % 2, :],
                                   [((hT_hi[:, k, rows], hT_lo[:, k, rows]), (w_hi["v"][:, k, :], w_lo["v"][:, k, :]))
                                    for k in range(KT)], part, parts)
                if mm:
                    mm.then_inc(v_made, 1)

            def o_rows(b, nt, part, parts):
                if part == 0:
                    if not (isinstance(b, int) and b == B - 1):
                        pe.wait_ge((q_lo_done, k_lo_done)[nt % 2], b * CHUNKS + (CHUNKS + 2 + nt // 2))
                    elif nt > 1:
                        pe.wait_ge(out_done, b * NT + (nt - 1))
                rows = slice(nt * P, (nt + 1) * P)
                mm = split_product(proj_ps[:, nt % 2, :],
                                   [((oT_hi[:, k, rows], oT_lo[:, k, rows]), (w_hi["o"][:, k, :], w_lo["o"][:, k, :]))
                                    for k in range(KT)], part, parts, (oT_lo_done, b * CHUNKS) if nt == 0 else None)
                if mm:
                    mm.then_inc(o_made, 1)

            def transpose_h(b, k):
                if k == 0:
                    pe.wait_ge(h_done, b * NT + NT)
                if k < 2:
                    if not (isinstance(b, int) and b == 0):
                        pe.wait_ge((q_lo_done, k_lo_done)[k], b * CHUNKS)
                else:
                    pe.wait_ge(hT_full_done, b * KT + (k - 1))
                for nt in range(NT):
                    mm = nc.tensor.transpose(proj_ps[:, k % 2, nt * P:(nt + 1) * P], rows[:, nt, k * P:(k + 1) * P],
                                             ident[:, :])
                mm.then_inc(hT_made, 1)

            def make_scores(b, u):
                c, nt, j = unit(u)
                if u % CU == 0:
                    pe.wait_ge(stack_in, b * (CHUNKS * STACK_DMAS * 16) + (u // CU + 1) * STACK_DMAS * 16)
                if not (isinstance(b, int) and b * UNITS + u < 2):
                    pe.wait_ge(neg_a, b * UNITS + (u - 1))
                nc.tensor.matmul(s_ps[:, u % 2, :], q_stack[c % 2][:, j, nt * P:(nt + 1) * P], k_stack[c % 2][:, j, :],
                                 start=True, stop=True).then_inc(scores, 1)

            def transpose_probs(b, u):
                pe.wait_ge(probs, b * UNITS + (u + 1))
                if not (isinstance(b, int) and b * UNITS + u < 2):
                    pe.wait_ge(pT_copied, b * UNITS + (u - 1))
                for m in range(NT):
                    mm = nc.tensor.transpose(t_ps[:, u % 2, m * P:(m + 1) * P], ring[:, u % RING, m * P:(m + 1) * P],
                                             ident[:, :])
                mm.then_inc(probs_T, 1)

            def spread_r(b, c):
                pe.wait_ge(r_done, b * CHUNKS + (c + 1))
                if not (isinstance(b, int) and b == 0 and c == 0):
                    pe.wait_ge(r_copied, b * CHUNKS + c)
                for nt in range(NT):
                    mm = nc.tensor.transpose(r_ps[:, nt * P:(nt + 1) * P],
                                             r_row[:, nt * PER:(nt + 1) * PER, :].rearrange("p j d -> p (j d)"),
                                             ident[:, :])
                mm.then_inc(r_T, 1)

            def weigh_v(b, p, part):
                c, half = divmod(p % PAIRS, 2)
                if part == 0:
                    pe.wait_ge(pT_copied, b * UNITS + (p + 1) * 2 * PER)
                    if half == 0 and not (isinstance(b, int) and b == 0 and p == 0):
                        pe.wait_ge(oT_done, b * CHUNKS + c)
                    if c == CHUNKS - 1 and half == 0:
                        pe.wait_ge(v_moved, b + 1)
                g = 2 * p % 4
                for m in (2 * part, 2 * part + 1):
                    for j in range(PER):
                        h = c * PER + j
                        mm = nc.tensor.matmul(o_ps[j * HD:(j + 1) * HD, half * 2 * P:(half + 1) * 2 * P],
                                              v_sb[:, m, h * HD:(h + 1) * HD], pT[:, g:g + 2, j, m * P:(m + 1) * P],
                                              start=(m == 0), stop=(m == NT - 1), skip_group_check=True)
                if part == 1:
                    mm.then_inc(pv, 1)

            def body(b, first=False, last=False, drain=False):
                for u in range(UNITS if not drain else sum(O_PLAN[-1])):
                    t = u % CU
                    if not drain and not (last and u == UNITS - 1):
                        make_scores(b, u + 1)
                    if not (first and u < LAG) and not (drain and u >= LAG):
                        transpose_probs(b, u - LAG)
                    if u % 8 in (3, 4) and not (first and u < 11) and not (drain and u > 4):
                        weigh_v(b, (u - 11) // 8, u % 8 - 3)
                    if t == 3 and not (first and u < CU) and not (drain and u > CU):
                        spread_r(b if u > CU else b - 1, (u // CU - 1) % CHUNKS)
                    for (c, which), (start, slots, _) in QK_PLAN.items():
                        if start <= u < start + slots and not drain and not (last and c == 0):
                            qk(b if c else b + 1, c, which, u - start, slots)
                    for nt, (start, slots) in enumerate(O_PLAN):
                        if start <= u < start + slots and not first:
                            o_rows(b - 1, nt, u - start, slots)
                    if not last and not drain:
                        if HT_SLOT <= u < HT_SLOT + KT:
                            transpose_h(b + 1, u - HT_SLOT)
                        for nt, (start, slots) in enumerate(V_PLAN):
                            if start <= u < start + slots:
                                v_rows(b + 1, nt, u - start, slots)

            pe.wait_ge(ident_ready, 2)
            for k in range(KT):
                transpose_h(0, k)
            pe.wait_ge(w_lo_done, 2)
            for which in "qk":
                for part in range(4):
                    qk(0, 0, which, part, 4)
            pe.wait_ge(w_lo_done, 4)
            for nt in range(NT):
                for part in range(2):
                    v_rows(0, nt, part, 2)
            make_scores(0, 0)
            samples(pe, body)

        @block.vector
        def _(dve):
            def split_w(n):
                k = "qkvo"[n]
                dve.wait_ge(w_hi_done, n + 1)
                nc.vector.tensor_tensor(w_lo[k][:, :, :], stage[:, n], f(w_hi[k][:, :, :]),
                                        ALU.subtract).then_inc(w_lo_done, 1)

            def copy_pT(b, u):
                c, nt, j = unit(u)
                g = u // PER
                dve.wait_ge(probs_T, b * UNITS + (u + 1))
                if j == 0 and not (isinstance(b, int) and b * GROUPS + g < 4):
                    dve.wait_ge(pv, b * PAIRS + (g - 2) // 2)
                nc.vector.tensor_copy(pT[:, g % 4, j, :], t_ps[:, u % 2, :]).then_inc(pT_copied, 1)

            def add_adj_and_max(b, u, wait):
                if wait:
                    dve.wait_ge(scores, b * UNITS + (u + 1))
                nc.vector.tensor_tensor_reduce(ring[:, u % RING, :], s_ps[:, u % 2, :], adj_sb[:, unit(u)[1], :], -2.0, 3e38,
                                               ALU.add, ALU.min, neg_max[:, u:u + 1]).then_inc(neg_a, 1)

            def row_stats(b, nt):
                dve.wait_ge(x_in[nt], b * 16 + 16)
                nc.vector.bn_stats(stats[:, nt, :], rows[:, nt, :]).then_inc(stats_done, 1)

            def aggregate(b):
                if isinstance(b, int):
                    dve.wait_ge(stats_done, b * NT + NT)
                for nt in range(NT):
                    nc.vector.bn_aggr(mean_var[:, nt, :], stats[:, nt, :]).then_inc(aggr_done, 1)

            def split_q(b, c):
                dve.wait_ge(q_hi_done, b * CHUNKS + (c + 1))
                nc.vector.scalar_tensor_tensor(out=q_lo, in0=proj_ps[:, 0, :], scalar=HALF_SCALE, in1=f(q_hi),
                                               op0=ALU.mult, op1=ALU.subtract).then_inc(q_lo_done, 1)

            def split_k(b, c):
                dve.wait_ge(k_hi_done, b * CHUNKS + (c + 1))
                nc.vector.tensor_tensor(k_lo, proj_ps[:, 1, :], f(k_hi), ALU.subtract).then_inc(k_lo_done, 1)

            def invert_sums(b, c):
                cols = slice(c * CU, (c + 1) * CU)
                n = b * (4 * CHUNKS) + 4 * c
                dve.wait_ge(probs, b * UNITS + (c + 1) * CU)
                if not (isinstance(b, int) and b == 0 and c == 0):
                    dve.wait_ge(r_done, b * CHUNKS + c)
                nc.vector.reciprocal(r_small[:, 0, :], row_sum[:, cols]).then_inc(r_step, 1)
                nc.vector.tensor_scalar(r_small[:, 1, :], neg_max[:, cols], 0.0, None, ALU.is_equal).then_inc(r_step, 1)
                dve.wait_ge(r_step, n + 2)
                nc.vector.scalar_tensor_tensor(out=r_small[:, 2, :], in0=row_sum[:, cols], scalar=float(N),
                                               in1=r_small[:, 1, :], op0=ALU.is_equal, op1=ALU.mult).then_inc(r_step, 1)
                dve.wait_ge(r_step, n + 3)
                nc.vector.tensor_scalar(r_small[:, 3, :], r_small[:, 2, :], 0.0, None, ALU.is_equal).then_inc(r_step, 1)

            def normalise_o(b, c):
                dve.wait_ge(r_copied, b * CHUNKS + (c + 1))
                dve.wait_ge(pv, b * PAIRS + (c + 1) * 2)
                nc.vector.tensor_tensor(oT[:, :], o_ps[:, :], oT[:, :], ALU.mult).then_inc(oT_done, 1)

            def move_v(b):
                dve.wait_ge(v_copied, (b + 1) * (2 * NT))
                if not (isinstance(b, int) and b == 0):
                    dve.wait_ge(pv, b * PAIRS)
                nc.vector.tensor_copy(v_sb[:, :, (CHUNKS - 1) * P:D], v_side[:, :, :]).then_inc(v_moved, 1)

            def add_residual(b, nt):
                if nt == 0:
                    dve.wait_ge(resid_in, b * 16 + 16)
                dve.wait_ge(o_made, b * NT + (nt + 1))
                nc.vector.tensor_tensor(rows[:, nt, :], proj_ps[:, nt % 2, :], rows[:, nt, :],
                                        ALU.add).then_inc(out_done, 1)

            def body(b, first=False, last=False, drain=False):
                for u in range(UNITS if not drain else sum(O_PLAN[-1]) + 1):
                    t = u % CU
                    if not drain:
                        add_adj_and_max(b, u, first and u <= LAG)
                    if u == STATS_PLAN[-1] + 1 and not last and not drain:
                        dve.wait_ge(stats_done, b * NT + 2 * NT)
                    if not last and u == UNITS - 1:
                        dve.wait_ge(adj_in[0], b * 16 + 32)
                    if not first and not drain and u in (PER - 1, 2 * PER - 1, 3 * PER - 1):
                        dve.wait_ge(adj_in[(u + 1) // PER], b * 16 + 16)
                    if not (first and u < LAG) and not (drain and u >= LAG):
                        copy_pT(b, u - LAG)
                    if t == 1 and not (first and u < CU) and not (drain and u > CU):
                        invert_sums(b if u > CU else b - 1, (u // CU - 1) % CHUNKS)
                    if t == 6 and not (first and u < CU) and not (drain and u > CU):
                        normalise_o(b if u > CU else b - 1, (u // CU - 1) % CHUNKS)
                    for (c, which), (_, _, rounded) in QK_PLAN.items():
                        if u == rounded + 1 and not drain and not (last and c == 0):
                            (split_q if which == "q" else split_k)(b if c else b + 1, c)
                    if u == 9 and not drain:
                        move_v(b)
                    for nt, (start, slots) in enumerate(O_PLAN):
                        if u == start + slots and not first:
                            add_residual(b - 1, nt)
                    if not last and not drain:
                        if u in STATS_PLAN:
                            row_stats(b + 1, STATS_PLAN.index(u))
                        if u == STATS_PLAN[-1] + 1:
                            aggregate(b + 1)

            for nt in range(NT):
                row_stats(0, nt)
            aggregate(0)
            split_w(0)
            split_w(1)
            split_q(0, 0)
            split_k(0, 0)
            split_w(2)
            split_w(3)
            for nt in range(NT):
                dve.wait_ge(adj_in[nt], 16)
            samples(dve, body)

        @block.scalar
        def _(act):
            def round_w(n):
                act.wait_ge(w_in[n], 16)
                nc.scalar.activation(w_hi["qkvo"[n]][:, :, :], stage[:, n], ACT.Copy).then_inc(w_hi_done, 1)

            def exponentials(b, u):
                act.wait_ge(neg_a, b * UNITS + (u + 1))
                nc.scalar.activation(ring[:, u % RING, :], ring[:, u % RING, :], ACT.Exp, bias=neg_max[:, u:u + 1],
                                     scale=-1.0, accum_out=row_sum[:, u:u + 1]).then_inc(probs, 1)

            def normalise(b, nt):
                act.wait_ge(rstd_done, b * 4 + 4)
                nc.scalar.activation(rows[:, nt, :], rows[:, nt, :], ACT.Identity, bias=shift[:, nt:nt + 1],
                                     scale=rstd[:, nt:nt + 1]).then_inc(h_done, 1)

            def round_hT(b, k):
                act.wait_ge(hT_made, b * KT + (k + 1))
                if k == 0 and not (isinstance(b, int) and b == 0):
                    act.wait_ge(k_made, b * CHUNKS)
                nc.scalar.activation(hT_hi[:, k, :], proj_ps[:, k % 2, :], ACT.Relu).then_inc(hT_hi_done, 1)
                if k:
                    act.wait_ge(hT_lo_done, b * KT + k)
                elif not (isinstance(b, int) and b == 0):
                    act.wait_ge(r_T, b * CHUNKS - 2)
                nc.scalar.activation(hT_full[:, :], proj_ps[:, k % 2, :], ACT.Relu).then_inc(hT_full_done, 1)

            def round_q(b, c):
                act.wait_ge(q_made, b * CHUNKS + (c + 1))
                if not (isinstance(b, int) and b == 0 and c == 0):
                    act.wait_ge(stack_in, b * (CHUNKS * STACK_DMAS * 16) + c * STACK_DMAS * 16)
                nc.scalar.activation(q_hi, proj_ps[:, 0, :], ACT.Copy, scale=HALF_SCALE).then_inc(q_hi_done, 1)

            def round_k(b, c):
                act.wait_ge(k_made, b * CHUNKS + (c + 1))
                nc.scalar.activation(k_hi, proj_ps[:, 1, :], ACT.Copy).then_inc(k_hi_done, 1)

            def copy_v(b, nt):
                act.wait_ge(v_made, b * NT + (nt + 1))
                if nt == 0 and not (isinstance(b, int) and b == 0):
                    act.wait_ge(pv, b * PAIRS - 2)
                    act.wait_ge(v_moved, b)
                cut = (CHUNKS - 1) * P
                nc.scalar.activation(v_sb[:, nt, 0:cut], proj_ps[:, nt % 2, 0:cut], ACT.Copy).then_inc(v_copied, 1)
                nc.scalar.activation(v_side[:, nt, :], proj_ps[:, nt % 2, cut:D], ACT.Copy).then_inc(v_copied, 1)

            def copy_r(b, c):
                act.wait_ge(r_T, b * CHUNKS + (c + 1))
                if not (isinstance(b, int) and b == 0 and c == 0):
                    act.wait_ge(oT_lo_done, b * CHUNKS + c)
                nc.scalar.activation(oT[:, :], r_ps[:, :], ACT.Copy).then_inc(r_copied, 1)

            def round_o(b, c):
                act.wait_ge(oT_done, b * CHUNKS + (c + 1))
                if c == 0 and not (isinstance(b, int) and b == 0):
                    act.wait_ge(o_made, b * NT)
                nc.scalar.activation(oT_hi[:, c, :], oT[:, :], ACT.Copy).then_inc(oT_hi_done, 1)

            def body(b, first=False, last=False, drain=False):
                for u in range(UNITS if not drain else CU):
                    t = u % CU
                    if not drain:
                        exponentials(b, u)
                    if t == 4 and not (first and u < CU):
                        copy_r(b if u > CU else b - 1, (u // CU - 1) % CHUNKS)
                    if t == 8 and not (first and u < CU):
                        round_o(b if u > CU else b - 1, (u // CU - 1) % CHUNKS)
                    for (c, which), (_, _, rounded) in QK_PLAN.items():
                        if u == rounded and not drain and not (last and c == 0):
                            (round_q if which == "q" else round_k)(b if c else b + 1, c)
                    if u == 0 and not first and not drain:
                        copy_v(b, NT - 1)
                    if not last and not drain:
                        for nt in range(NT):
                            if u == NORMALISE_PLAN[nt]:
                                normalise(b + 1, nt)
                        if HT_SLOT <= u < HT_SLOT + KT:
                            round_hT(b + 1, u - HT_SLOT)
                        for nt in range(NT - 1):
                            if u == sum(V_PLAN[nt]):
                                copy_v(b + 1, nt)

            for nt in range(NT):
                normalise(0, nt)
            round_w(0)
            round_w(1)
            for k in range(KT):
                round_hT(0, k)
            round_q(0, 0)
            round_k(0, 0)
            round_w(2)
            round_w(3)
            for nt in range(NT):
                copy_v(0, nt)
            samples(act, body)

        @block.gpsimd
        def _(pool):
            nc.gpsimd.memset(ident[:, :], 0.0).then_inc(ident_ready, 1)
            nc.gpsimd.memset(consts[:, 0, :], EPS).then_inc(consts_ready, 1)
            nc.gpsimd.memset(consts[:, 1, :], -0.5).then_inc(consts_ready, 1)
            nc.gpsimd.memset(consts[:, 2, :], -1.0).then_inc(consts_ready, 1)
            pool.wait_ge(ident_ready, 1)
            nc.gpsimd.affine_select(out=ident[:, :], in_=ident[:, :], compare_op=ALU.not_equal, fill=1.0, base=0,
                                    pattern=[[-1, P]], channel_multiplier=1).then_inc(ident_ready, 1)

            def inverse_deviation(b):
                pool.wait_ge(aggr_done, b * NT + NT)
                nc.gpsimd.tensor_tensor(var_eps[:, :], mean_var[:, :, 1], consts[:, 0, :], ALU.add).then_inc(rstd_done, 1)
                pool.wait_ge(rstd_done, b * 4 + 1)
                nc.gpsimd.tensor_tensor(rstd[:, :], var_eps[:, :], consts[:, 1, :], ALU.pow).then_inc(rstd_done, 1)
                pool.wait_ge(rstd_done, b * 4 + 2)
                nc.gpsimd.tensor_tensor(var_eps[:, :], rstd[:, :], consts[:, 2, :], ALU.mult).then_inc(rstd_done, 1)
                pool.wait_ge(rstd_done, b * 4 + 3)
                nc.gpsimd.tensor_tensor(shift[:, :], mean_var[:, :, 0], var_eps[:, :], ALU.mult).then_inc(rstd_done, 1)

            def split_hT(b, k):
                pool.wait_ge(hT_full_done, b * KT + (k + 1))
                nc.gpsimd.tensor_tensor(hT_lo[:, k, :], hT_full[:, :], f(hT_hi[:, k, :]), ALU.subtract).then_inc(hT_lo_done, 1)

            def repeat_r(b, c):
                pool.wait_ge(r_step, b * (4 * CHUNKS) + 4 * (c + 1))
                if not (isinstance(b, int) and b == 0 and c == 0):
                    pool.wait_ge(r_T, b * CHUNKS + c)
                nc.gpsimd.tensor_tensor(r_row[:, :, :], r_small[:, 0, :].unsqueeze(2).to_broadcast([P, CU, HD]),
                                        r_small[:, 3, :].unsqueeze(2).to_broadcast([P, CU, HD]),
                                        ALU.mult).then_inc(r_done, 1)

            def split_o(b, c):
                pool.wait_ge(oT_hi_done, b * CHUNKS + (c + 1))
                nc.gpsimd.tensor_tensor(oT_lo[:, c, :], oT[:, :], f(oT_hi[:, c, :]), ALU.subtract).then_inc(oT_lo_done, 1)

            def body(b, first=False, last=False, drain=False):
                for c in range(CHUNKS if not drain else 1):
                    if c == 2 and not last and not drain:
                        inverse_deviation(b + 1)
                    if not (first and c == 0):
                        repeat_r(b if c else b - 1, (c - 1) % CHUNKS)
                    if c == 2 and not last and not drain:
                        for k in range(2):
                            split_hT(b + 1, k)
                    if not (first and c == 0):
                        split_o(b if c else b - 1, (c - 1) % CHUNKS)
                    if c == 2 and not last and not drain:
                        for k in range(2, KT):
                            split_hT(b + 1, k)

            pool.wait_ge(consts_ready, 3)
            inverse_deviation(0)
            for k in range(KT):
                split_hT(0, k)
            samples(pool, body)


_INS = ["x", "adj", "wq_t", "wk_t", "wv_t", "wo_t"]


def kernel(x, adj, L0_gnn_Wq, L0_gnn_Wk, L0_gnn_Wv, L0_gnn_Wo):
    import numpy as np
    import concourse.bacc as bacc
    from concourse import mybir as mb
    from concourse.bass_utils import run_bass_kernel_spmd

    given = dict(zip(_INS, (x, adj, *(np.asarray(w).T for w in (L0_gnn_Wq, L0_gnn_Wk, L0_gnn_Wv, L0_gnn_Wo)))))
    nc = bacc.Bacc("TRN2", target_bir_lowering=False, num_devices=1)
    arrays, args = {}, []
    for name in _INS:
        a = np.ascontiguousarray(given[name])
        arrays[f"in_{name}"] = a
        args.append(nc.dram_tensor(f"in_{name}", a.shape, mb.dt.from_np(a.dtype), kind="ExternalInput").ap())
    shape = tuple(np.asarray(x).shape)
    args.append(nc.dram_tensor("out_0", shape, mb.dt.from_np(np.dtype("float32")), kind="ExternalOutput").ap())
    graph_attention(nc, *args)
    r = run_bass_kernel_spmd(nc, [arrays], core_ids=[0])
    return r.results[0]["out_0"]
```

```python
from contextlib import ExitStack

import concourse.bass as bass
from concourse import mybir

ALU = mybir.AluOpType
ACT = mybir.ActivationFunctionType
F32 = mybir.dt.float32
F32R = mybir.dt.float32r

P = 128
HEADS = 16
EPS = 1e-5
LAG = 3
RING = LAG + 1

QK_PLAN = {(1, "q"): ((0, 1, 2, 3), 3, 4), (1, "k"): ((4, 5, 6, 7), 7, 8),
           (2, "k"): ((11, 12, 13), 15, 16), (2, "q"): ((14, 15, 16), 16, 18),
           (3, "q"): ((28, 29, 30), 30, 31), (3, "k"): ((31, 32, 33, 34), 34, 35),
           (0, "q"): ((39, 40, 41, 42), 42, 43), (0, "k"): ((43, 44, 45, 46), 46, 47)}
O_PLAN = (((8, 9, 10), 11), ((17, 18, 19), 20), ((20, 21, 22, 23), 24), ((24, 25, 26, 27), 30))
LAST_O_EARLY = ((57, 58, 59), (60, 61, 62), (0, 1, 2), (5, 6, 7))
LAST_O = (8, 9, 10, 11)
STATS_PLAN = (27, 28, 23, 25)
AGGREGATE_SLOT = 29
NORMALISE_PLAN = (30, 31, 32, 33)
HT_SLOT = 35
NORMALISE_O_PLAN = (21, 40, 53, 5)
ROUND_O_PLAN = (28, 42, 55, 7)
ACT_COPY_SLOTS = (1, 4, 5, 8, 11, 17, 20, 21, 23, 24, 25, 27, 28, 31, 35, 36, 37, 38, 40, 43, 47, 49, 53)
V_PLAN = ((47, 4), (51, 4), (55, 4), (59, 4))
V_COPY_PLAN = (53, 55, 59)
MOVE_V_SLOT = 7


def graph_attention(nc, x, adj, wq_t, wk_t, wv_t, wo_t, out):
    B, N, D = x.shape
    HD = D // HEADS
    NT = N // P
    KT = D // P
    PER = P // HD
    CHUNKS = HEADS // PER
    UNITS = HEADS * NT
    CU = UNITS // CHUNKS
    GROUPS = UNITS // PER
    PAIRS = GROUPS // 2
    HALF_SCALE = 0.5 * float(D) ** -0.5
    STACK_DMAS = 3 * PER
    assert (N, D, HD, NT, KT, PER, CHUNKS, CU) == (512, 512, 32, 4, 4, 4, 4, 16)

    with ExitStack() as ctx:
        def sb(name, shape, dt=F32):
            return ctx.enter_context(nc.sbuf_tensor(name, shape, dt))

        def ps(name, shape):
            return ctx.enter_context(nc.psum_tensor(name, shape, F32))

        def sem(name):
            return ctx.enter_context(nc.semaphore(name))

        w_hi = {k: sb(f"w{k}_hi", [P, KT, D], F32R) for k in "qkvo"}
        w_lo = {k: sb(f"w{k}_lo", [P, KT, D], F32R) for k in "qkvo"}
        qk_stack = [sb(f"qk_stack{i}", [3 * HD, 2, PER, N], F32R) for i in range(2)]
        q_stack = [stack[:, 0] for stack in qk_stack]
        k_stack = [stack[:, 1] for stack in qk_stack]
        qk_parts = sb("qk_parts", [P, 4, N], F32R)
        q_lo, q_hi, k_hi, k_lo = (qk_parts[:, i, :] for i in range(4))
        hT_hi = sb("hT_hi", [P, KT, N], F32R)
        hT_lo = sb("hT_lo", [P, KT, N], F32R)
        rows = sb("rows", [P, NT, D])
        adj_sb = sb("adj_sb", [P, NT, N])
        v_sb = sb("v_sb", [P, NT, D])
        v_side = sb("v_side", [P, NT, P])
        ring = sb("ring", [P, RING, N])
        pT = sb("pT", [P, 4, PER, N])
        oT = sb("oT", [P, N])
        oT_hi = sb("oT_hi", [P, CHUNKS, N], F32R)
        oT_lo = sb("oT_lo", [P, CHUNKS, N], F32R)
        ident = sb("ident", [P, P])
        stats = sb("stats", [P, NT, 6])
        mean_var = sb("mean_var", [P, NT, 2])
        var_eps = sb("var_eps", [P, NT])
        rstd = sb("rstd", [P, NT])
        shift = sb("shift", [P, NT])
        consts = sb("consts", [P, 3, NT])
        neg_max = sb("neg_max", [P, UNITS])
        row_sum = sb("row_sum", [P, UNITS])
        r_small = sb("r_small", [P, 4, CU])
        r_row = sb("r_row", [P, CU, HD])
        stage = pT

        s_ps = ps("s_ps", [P, 2, N])
        t_ps = ps("t_ps", [P, 2, N])
        o_ps = ps("o_ps", [P, N])
        proj_ps = ps("proj_ps", [P, 2, N])
        r_ps = ps("r_ps", [P, N])

        ident_ready = sem("ident_ready")
        consts_ready = sem("consts_ready")
        w_in = [sem(f"w_in{i}") for i in range(4)]
        w_hi_done = {k: sem(f"w{k}_hi_done") for k in "qkvo"}
        w_lo_done = {k: sem(f"w{k}_lo_done") for k in "qkvo"}
        x_in = [sem(f"x_in{nt}") for nt in range(NT)]
        adj_in = [sem(f"adj_in{nt}") for nt in range(NT)]
        stats_done = sem("stats_done")
        aggr_done = sem("aggr_done")
        rstd_done = sem("rstd_done")
        h_done = sem("h_done")
        hT_made = sem("hT_made")
        hT_hi_done = sem("hT_hi_done")
        hT_lo_done = sem("hT_lo_done")
        q_made = sem("q_made")
        k_made = sem("k_made")
        q_hi_done = sem("q_hi_done")
        k_hi_done = sem("k_hi_done")
        q_lo_done = sem("q_lo_done")
        k_lo_done = sem("k_lo_done")
        stack_in = sem("stack_in")
        v_made = sem("v_made")
        v_copied = sem("v_copied")
        v_moved = sem("v_moved")
        scores = sem("scores")
        neg_a = sem("neg_a")
        probs = sem("probs")
        probs_T = sem("probs_T")
        pT_copied = sem("pT_copied")
        pT_copied_act = sem("pT_copied_act")
        pv = sem("pv")
        r_step = sem("r_step")
        r_done = sem("r_done")
        r_T = sem("r_T")
        r_copied = sem("r_copied")
        oT_done = sem("oT_done")
        oT_hi_done = sem("oT_hi_done")
        oT_lo_done = sem("oT_lo_done")
        o_made = sem("o_made")
        out_done = sem("out_done")
        resid_in = [sem(f"resid_in{nt}") for nt in range(NT)]
        stored = [sem(f"stored{nt}") for nt in range(NT)]

        x_t = x.rearrange("b (t p) d -> b p t d", p=P)
        adj_t = adj.rearrange("b (t p) m -> b p t m", p=P)
        out_t = out.rearrange("b (t p) d -> b p t d", p=P)

        def f(ap):
            return ap.bitcast(F32)

        def copies(b, u):
            turns, slot = divmod(u + LAG, UNITS)
            act = turns * len(ACT_COPY_SLOTS) + sum(s <= slot for s in ACT_COPY_SLOTS)
            act -= sum(s < LAG for s in ACT_COPY_SLOTS)
            return b * (UNITS - len(ACT_COPY_SLOTS)) + (u + 1 - act), b * len(ACT_COPY_SLOTS) + act

        def copied_by_act(u):
            return (u + LAG) % UNITS in ACT_COPY_SLOTS

        def last_sample(b):
            return isinstance(b, int) and b == B - 1

        def o_bank(b, nt):
            return (proj_ps, s_ps)[nt // 2][:, nt % 2, :] if last_sample(b) else proj_ps[:, nt % 2, :]

        def o_tile(b, nt):
            if nt < (3 if last_sample(b) else 2):
                return rows[:, nt, :]
            return v_side[:, :, :].rearrange("p t d -> p (t d)")

        def unit(u):
            c, rest = divmod(u % UNITS, CU)
            nt, j = divmod(rest, PER)
            return c, nt, j

        def samples(eng, body):
            body(0, first=True)
            with eng.Fori(1, B - 1) as b:
                body(b)
            body(B - 1, last=True)
            body(B, drain=True)

        block = ctx.enter_context(nc.Block())

        @block.sync
        def _(sp):
            def load_x(b, nt):
                sp.dma_start(rows[:, nt, :], x_t[b][:, nt, :]).then_inc(x_in[nt], 16)

            def load_adj(b, nt):
                if not (isinstance(b, int) and b == 0):
                    sp.wait_ge(neg_a, b * UNITS + ((nt + 1) * PER - CU))
                sp.dma_start(adj_sb[:, nt, :], adj_t[b][:, nt, :]).then_inc(adj_in[nt], 16)

            def fill_stack(b, c):
                n = b * CHUNKS + (c + 1)
                sp.wait_ge(q_lo_done, n)
                sp.wait_ge(k_lo_done, n)
                for row, parts in enumerate((slice(1, 3), slice(0, 3, 2), slice(1, 4, 2))):
                    for j in range(PER):
                        sp.dma_start(f(qk_stack[c % 2][row * HD:(row + 1) * HD, :, j, :]),
                                     f(qk_parts[j * HD:(j + 1) * HD, parts, :])).then_inc(stack_in, 16)

            def load_residual(b, nt):
                sp.dma_start(o_tile(b, nt), x_t[b][:, nt, :]).then_inc(resid_in[nt], 16)

            def store(b, nt):
                sp.wait_ge(out_done, b * NT + (nt + 1))
                sp.dma_start(out_t[b][:, nt, :], o_tile(b, nt)).then_inc(stored[nt], 16)

            def body(b, first=False, last=False, drain=False):
                if drain:
                    for nt in range(NT):
                        sp.wait_ge(stored[nt], (b - 1) * 16)
                        load_residual(b - 1, nt)
                    for nt in range(NT):
                        store(b - 1, nt)
                    return
                sp.wait_ge(hT_made, b * KT + KT)
                if not first:
                    load_residual(b - 1, 0)
                    load_residual(b - 1, 1)
                if not last:
                    load_x(b + 1, 2)
                    load_x(b + 1, 3)
                fill_stack(b, 1)
                if not first:
                    store(b - 1, 0)
                    load_residual(b - 1, 2)
                fill_stack(b, 2)
                if not first:
                    store(b - 1, 1)
                    for nt in (0, 1):
                        sp.wait_ge(stored[nt], b * 16)
                if not last:
                    load_x(b + 1, 1)
                    load_x(b + 1, 0)
                if not first:
                    store(b - 1, 2)
                    sp.wait_ge(stored[2], b * 16)
                    load_residual(b - 1, 3)
                    store(b - 1, 3)
                fill_stack(b, 3)
                if not last:
                    fill_stack(b + 1, 0)
                    for nt in range(NT):
                        load_adj(b + 1, nt)

            for nt in range(NT):
                load_x(0, nt)
            for n, w in enumerate((wq_t, wk_t, wv_t, wo_t)):
                sp.dma_start(stage[:, n], w.rearrange("(t p) n -> p t n", p=P)).then_inc(w_in[n], 16)
            for nt in range(NT):
                load_adj(0, nt)
            fill_stack(0, 0)
            samples(sp, body)
            for nt in range(NT):
                sp.wait_ge(stored[nt], B * 16)

        @block.tensor
        def _(pe):
            def split_product(out_ps, pairs, part, parts, wait=None):
                steps = [(l, r) for lhs, rhs in pairs for l, r in ((lhs[0], rhs[0]), (lhs[1], rhs[0]), (lhs[0], rhs[1]))]
                assert len(steps) % parts == 0
                share = len(steps) // parts
                if wait:
                    done, base = wait
                    pe.wait_ge(done, base + (((part + 1) * share - 1) // 3 + 1))
                for i in range(part * share, (part + 1) * share):
                    mm = nc.tensor.matmul(out_ps, steps[i][0], steps[i][1], start=(i == 0), stop=(i == len(steps) - 1))
                return mm if part == parts - 1 else None

            def qk(b, c, which, part, parts):
                bank = "qk".index(which)
                if part == 0:
                    if c == 0:
                        pe.wait_ge(hT_lo_done, b * KT + (KT - 1 + bank))
                        if isinstance(b, int) and b == 0:
                            pe.wait_ge(w_lo_done[which], 1)
                    elif c == 1:
                        pe.wait_ge(v_copied, b * (2 * NT) + 2 * (NT - 1 + bank))
                    elif (c, which) == (2, "k") or isinstance(b, int) and b == 0:
                        pe.wait_ge((q_lo_done, k_lo_done)[bank], b * CHUNKS + c)
                    else:
                        tile = {(2, "q"): 0, (3, "q"): 2, (3, "k"): 3}[c, which]
                        pe.wait_ge(out_done, b * NT + (tile + 1 - NT))
                cols = slice(c * P, (c + 1) * P)
                mm = split_product(proj_ps[:, bank, :],
                                   [((w_hi[which][:, k, cols], w_lo[which][:, k, cols]), (hT_hi[:, k, :], hT_lo[:, k, :]))
                                    for k in range(KT)], part, parts, (hT_lo_done, b * KT) if c == 0 else None)
                if mm:
                    mm.then_inc((q_made, k_made)[bank], 1)

            def v_rows(b, nt, part, parts):
                if part == 0:
                    if nt < 2:
                        pe.wait_ge((q_lo_done, k_lo_done)[nt], b * CHUNKS + 1)
                    else:
                        pe.wait_ge(v_copied, b * (2 * NT) + 2 * (nt - 1))
                rows = slice(nt * P, (nt + 1) * P)
                mm = split_product(proj_ps[:, nt % 2, :],
                                   [((hT_hi[:, k, rows], hT_lo[:, k, rows]), (w_hi["v"][:, k, :], w_lo["v"][:, k, :]))
                                    for k in range(KT)], part, parts)
                if mm:
                    mm.then_inc(v_made, 1)

            def o_rows(b, nt, part, parts):
                if part == 0:
                    if last_sample(b):
                        if nt < 2:
                            pe.wait_ge((q_lo_done, k_lo_done)[nt], B * CHUNKS)
                        else:
                            pe.wait_ge(neg_a, B * UNITS + (nt - NT + 1))
                    elif nt == 3:
                        pe.wait_ge(out_done, b * NT + 2)
                    else:
                        pe.wait_ge((q_lo_done, k_lo_done)[nt % 2], b * CHUNKS + (CHUNKS + (2, 3, 3)[nt]))
                rows = slice(nt * P, (nt + 1) * P)
                mm = split_product(o_bank(b, nt),
                                   [((oT_hi[:, k, rows], oT_lo[:, k, rows]), (w_hi["o"][:, k, :], w_lo["o"][:, k, :]))
                                    for k in range(KT)], part, parts, (oT_lo_done, b * CHUNKS) if nt == 0 else None)
                if mm:
                    mm.then_inc(o_made, 1)

            def transpose_h(b, k):
                if k == 0:
                    pe.wait_ge(h_done, b * NT + NT)
                if k > 1:
                    pe.wait_ge(hT_lo_done, b * KT + (k - 1))
                elif not (isinstance(b, int) and b == 0):
                    pe.wait_ge((q_lo_done, k_lo_done)[k], b * CHUNKS)
                for nt in range(NT):
                    mm = nc.tensor.transpose(proj_ps[:, k % 2, nt * P:(nt + 1) * P], rows[:, nt, k * P:(k + 1) * P],
                                             ident[:, :])
                mm.then_inc(hT_made, 1)

            def make_scores(b, u):
                c, nt, j = unit(u)
                if u % CU == 0:
                    pe.wait_ge(stack_in, b * (CHUNKS * STACK_DMAS * 16) + (u // CU + 1) * STACK_DMAS * 16)
                if not (isinstance(b, int) and b * UNITS + u < 2):
                    pe.wait_ge(neg_a, b * UNITS + (u - 1))
                nc.tensor.matmul(s_ps[:, u % 2, :], q_stack[c % 2][:, j, nt * P:(nt + 1) * P], k_stack[c % 2][:, j, :],
                                 start=True, stop=True).then_inc(scores, 1)

            def transpose_probs(b, u):
                pe.wait_ge(probs, b * UNITS + (u + 1))
                if not (isinstance(b, int) and b * UNITS + u < 2):
                    by_act = copied_by_act(u - 2)
                    pe.wait_ge(pT_copied_act if by_act else pT_copied, copies(b, u - 2)[by_act])
                for m in range(NT):
                    mm = nc.tensor.transpose(t_ps[:, u % 2, m * P:(m + 1) * P], ring[:, u % RING, m * P:(m + 1) * P],
                                             ident[:, :])
                mm.then_inc(probs_T, 1)

            def spread_r(b, c):
                pe.wait_ge(r_done, b * CHUNKS + (c + 1))
                if not (isinstance(b, int) and b == 0 and c == 0):
                    pe.wait_ge(r_copied, b * CHUNKS + c)
                for nt in range(NT):
                    mm = nc.tensor.transpose(r_ps[:, nt * P:(nt + 1) * P],
                                             r_row[:, nt * PER:(nt + 1) * PER, :].rearrange("p j d -> p (j d)"),
                                             ident[:, :])
                mm.then_inc(r_T, 1)

            def weigh_v(b, p, part):
                c, half = divmod(p % PAIRS, 2)
                if part == 0:
                    for copied, n in zip((pT_copied, pT_copied_act), copies(b, (p + 1) * 2 * PER - 1)):
                        pe.wait_ge(copied, n)
                    if half == 0 and not (isinstance(b, int) and b == 0 and p == 0):
                        pe.wait_ge(oT_done, b * CHUNKS + c)
                    if c == CHUNKS - 1 and half == 0:
                        pe.wait_ge(v_moved, b + 1)
                g = 2 * p % 4
                for m in (2 * part, 2 * part + 1):
                    for j in range(PER):
                        h = c * PER + j
                        mm = nc.tensor.matmul(o_ps[j * HD:(j + 1) * HD, half * 2 * P:(half + 1) * 2 * P],
                                              v_sb[:, m, h * HD:(h + 1) * HD], pT[:, g:g + 2, j, m * P:(m + 1) * P],
                                              start=(m == 0), stop=(m == NT - 1), skip_group_check=True)
                if part == 1:
                    mm.then_inc(pv, 1)

            def body(b, first=False, last=False, drain=False):
                for u in range(UNITS if not drain else LAST_O[-1] + 1):
                    t = u % CU
                    if not drain and not (last and u == UNITS - 1):
                        make_scores(b, u + 1)
                    if not (first and u < LAG) and not (drain and u >= LAG):
                        transpose_probs(b, u - LAG)
                    if t == 3 and not (first and u < CU):
                        spread_r(b if u > CU else b - 1, (u // CU - 1) % CHUNKS)
                    if u % 8 in (3, 4) and not (first and u < 11) and not (drain and u > 4):
                        weigh_v(b, (u - 11) // 8, u % 8 - 3)
                    if not drain:
                        for (c, which), (slots, _, _) in QK_PLAN.items():
                            if u in slots and not (last and c == 0):
                                qk(b if c else b + 1, c, which, slots.index(u), len(slots))
                        for nt in range(NT):
                            slots, _ = O_PLAN[nt]
                            if u in slots and not first:
                                o_rows(b - 1, nt, slots.index(u), len(slots))
                            if u in LAST_O_EARLY[nt] and last and nt < 2:
                                o_rows(b, nt, LAST_O_EARLY[nt].index(u), KT)
                    else:
                        for nt in range(NT):
                            if u in LAST_O_EARLY[nt] and nt > 1:
                                o_rows(b - 1, nt, LAST_O_EARLY[nt].index(u), KT)
                            if u == LAST_O[nt]:
                                o_rows(b - 1, nt, KT - 1, KT)
                    if not last and not drain:
                        if HT_SLOT <= u < HT_SLOT + KT:
                            transpose_h(b + 1, u - HT_SLOT)
                        for nt, (start, slots) in enumerate(V_PLAN):
                            if start <= u < start + slots:
                                v_rows(b + 1, nt, u - start, slots)
                    if first and u == UNITS - 1:
                        pe.wait_ge(w_lo_done["o"], 1)

            pe.wait_ge(ident_ready, 2)
            for k in range(KT):
                transpose_h(0, k)
            for which in "qk":
                for part in range(4):
                    qk(0, 0, which, part, 4)
            pe.wait_ge(w_lo_done["v"], 1)
            for nt in range(NT):
                for part in range(2):
                    v_rows(0, nt, part, 2)
            make_scores(0, 0)
            samples(pe, body)

        @block.vector
        def _(dve):
            def split_w(n):
                k = "qkvo"[n]
                dve.wait_ge(w_hi_done[k], 1)
                nc.vector.tensor_tensor(w_lo[k][:, :, :], stage[:, n], f(w_hi[k][:, :, :]),
                                        ALU.subtract).then_inc(w_lo_done[k], 1)

            def split_hT(b, k):
                dve.wait_ge(hT_hi_done, b * KT + (k + 1))
                nc.vector.scalar_tensor_tensor(out=hT_lo[:, k, :], in0=proj_ps[:, k % 2, :], scalar=0.0,
                                               in1=f(hT_hi[:, k, :]), op0=ALU.max,
                                               op1=ALU.subtract).then_inc(hT_lo_done, 1)

            def copy_pT(b, u):
                c, nt, j = unit(u)
                g = u // PER
                dve.wait_ge(probs_T, b * UNITS + (u + 1))
                if j == 0 and isinstance(b, int) and b * GROUPS + g == 3:
                    dve.wait_ge(w_lo_done["o"], 1)
                if j == 0 and not (isinstance(b, int) and b * GROUPS + g < 4):
                    dve.wait_ge(pv, b * PAIRS + (g - 2) // 2)
                nc.vector.tensor_copy(pT[:, g % 4, j, :], t_ps[:, u % 2, :]).then_inc(pT_copied, 1)

            def add_adj_and_max(b, u, wait):
                if wait:
                    dve.wait_ge(scores, b * UNITS + (u + 1))
                nc.vector.tensor_tensor_reduce(ring[:, u % RING, :], s_ps[:, u % 2, :], adj_sb[:, unit(u)[1], :], -2.0, 3e38,
                                               ALU.add, ALU.min, neg_max[:, u:u + 1]).then_inc(neg_a, 1)

            def row_stats(b, nt):
                dve.wait_ge(x_in[nt], b * 16 + 16)
                nc.vector.bn_stats(stats[:, nt, :], rows[:, nt, :]).then_inc(stats_done, 1)

            def aggregate(b):
                if isinstance(b, int):
                    dve.wait_ge(stats_done, b * NT + NT)
                for nt in range(NT):
                    nc.vector.bn_aggr(mean_var[:, nt, :], stats[:, nt, :]).then_inc(aggr_done, 1)

            def split_q(b, c):
                dve.wait_ge(q_hi_done, b * CHUNKS + (c + 1))
                nc.vector.scalar_tensor_tensor(out=q_lo, in0=proj_ps[:, 0, :], scalar=HALF_SCALE, in1=f(q_hi),
                                               op0=ALU.mult, op1=ALU.subtract).then_inc(q_lo_done, 1)

            def split_k(b, c):
                dve.wait_ge(k_hi_done, b * CHUNKS + (c + 1))
                nc.vector.tensor_tensor(k_lo, proj_ps[:, 1, :], f(k_hi), ALU.subtract).then_inc(k_lo_done, 1)

            def invert_sums(b, c):
                cols = slice(c * CU, (c + 1) * CU)
                n = b * (4 * CHUNKS) + 4 * c
                dve.wait_ge(probs, b * UNITS + (c + 1) * CU)
                if not (isinstance(b, int) and b == 0 and c == 0):
                    dve.wait_ge(r_done, b * CHUNKS + c)
                nc.vector.reciprocal(r_small[:, 0, :], row_sum[:, cols]).then_inc(r_step, 1)
                nc.vector.tensor_scalar(r_small[:, 1, :], neg_max[:, cols], 0.0, None, ALU.is_equal).then_inc(r_step, 1)
                dve.wait_ge(r_step, n + 2)
                nc.vector.scalar_tensor_tensor(out=r_small[:, 2, :], in0=row_sum[:, cols], scalar=float(N),
                                               in1=r_small[:, 1, :], op0=ALU.is_equal, op1=ALU.mult).then_inc(r_step, 1)
                dve.wait_ge(r_step, n + 3)
                nc.vector.tensor_scalar(r_small[:, 3, :], r_small[:, 2, :], 0.0, None, ALU.is_equal).then_inc(r_step, 1)

            def normalise_o(b, c):
                dve.wait_ge(r_copied, b * CHUNKS + (c + 1))
                dve.wait_ge(pv, b * PAIRS + (c + 1) * 2)
                nc.vector.tensor_tensor(oT[:, :], o_ps[:, :], oT[:, :], ALU.mult).then_inc(oT_done, 1)

            def move_v(b):
                dve.wait_ge(v_copied, (b + 1) * (2 * NT))
                if not (isinstance(b, int) and b == 0):
                    dve.wait_ge(pv, b * PAIRS)
                nc.vector.tensor_copy(v_sb[:, :, (CHUNKS - 1) * P:D], v_side[:, :, :]).then_inc(v_moved, 1)

            def add_residual(b, nt):
                dve.wait_ge(resid_in[nt], b * 16 + 16)
                dve.wait_ge(o_made, b * NT + (nt + 1))
                nc.vector.tensor_tensor(o_tile(b, nt), o_bank(b, nt), o_tile(b, nt), ALU.add).then_inc(out_done, 1)

            def body(b, first=False, last=False, drain=False):
                for u in range(UNITS if not drain else LAST_O[-1] + 2):
                    t = u % CU
                    if isinstance(b, int) and (u - 1) in ACT_COPY_SLOTS and not drain and not (first and u <= LAG):
                        dve.wait_ge(probs_T, b * UNITS + (u - LAG))
                    if not drain:
                        add_adj_and_max(b, u, first and u <= LAG)
                    if u == AGGREGATE_SLOT and not last and not drain:
                        dve.wait_ge(stats_done, b * NT + 2 * NT)
                    if not last and u == UNITS - 1:
                        dve.wait_ge(adj_in[0], b * 16 + 32)
                    if not first and not drain and u in (PER - 1, 2 * PER - 1, 3 * PER - 1):
                        dve.wait_ge(adj_in[(u + 1) // PER], b * 16 + 16)
                    if u in ACT_COPY_SLOTS:
                        if not isinstance(b, int):
                            dve.wait_ge(probs_T, b * UNITS + (u - LAG + 1))
                    elif not (first and u < LAG) and not (drain and u >= LAG):
                        copy_pT(b, u - LAG)
                    if t == 1 and not (first and u < CU) and not (drain and u > CU):
                        invert_sums(b if u > CU else b - 1, (u // CU - 1) % CHUNKS)
                    if u in NORMALISE_O_PLAN and not (first and u < CU):
                        normalise_o(b if u > CU else b - 1, (u // CU - 1) % CHUNKS)
                    for (c, which), (_, _, split) in QK_PLAN.items():
                        if u == split and not drain and not (last and c == 0):
                            (split_q if which == "q" else split_k)(b if c else b + 1, c)
                    if u == MOVE_V_SLOT and not drain:
                        move_v(b)
                    for nt in range(NT):
                        if u == (LAST_O[nt] + 1 if drain else O_PLAN[nt][1]) and not first:
                            add_residual(b - 1, nt)
                    if not last and not drain:
                        if u in STATS_PLAN:
                            row_stats(b + 1, STATS_PLAN.index(u))
                        if HT_SLOT < u <= HT_SLOT + KT:
                            split_hT(b + 1, u - HT_SLOT - 1)
                        if u == AGGREGATE_SLOT:
                            aggregate(b + 1)

            for nt in range(NT):
                row_stats(0, nt)
            aggregate(0)
            dve.wait_ge(w_in[0], 16)
            nc.vector.tensor_copy(w_hi["q"][:, :, :], stage[:, 0]).then_inc(w_hi_done["q"], 1)
            split_w(0)
            for k in range(KT):
                split_hT(0, k)
            split_w(1)
            split_w(2)
            split_q(0, 0)
            split_k(0, 0)
            for nt in range(NT):
                dve.wait_ge(adj_in[nt], 16)
            samples(dve, body)

        @block.scalar
        def _(act):
            def round_w(n):
                act.wait_ge(w_in[n], 16)
                k = "qkvo"[n]
                nc.scalar.activation(w_hi[k][:, :, :], stage[:, n], ACT.Copy).then_inc(w_hi_done[k], 1)

            def exponentials(b, u):
                act.wait_ge(neg_a, b * UNITS + (u + 1))
                nc.scalar.activation(ring[:, u % RING, :], ring[:, u % RING, :], ACT.Exp, bias=neg_max[:, u:u + 1],
                                     scale=-1.0, accum_out=row_sum[:, u:u + 1]).then_inc(probs, 1)

            def copy_pT(b, u):
                g = u // PER
                act.wait_ge(probs_T, b * UNITS + (u + 1))
                if isinstance(b, int) and b == 0 and g < 4:
                    act.wait_ge(w_lo_done["qkvo"[g]], 1)
                else:
                    act.wait_ge(pv, b * PAIRS + (g - 2) // 2)
                nc.scalar.activation(pT[:, g % 4, u % PER, :], t_ps[:, u % 2, :], ACT.Copy).then_inc(pT_copied_act, 1)

            def normalise(b, nt):
                act.wait_ge(rstd_done, b * 4 + 4)
                nc.scalar.activation(rows[:, nt, :], rows[:, nt, :], ACT.Identity, bias=shift[:, nt:nt + 1],
                                     scale=rstd[:, nt:nt + 1]).then_inc(h_done, 1)

            def round_hT(b, k):
                act.wait_ge(hT_made, b * KT + (k + 1))
                if k == 0 and not (isinstance(b, int) and b == 0):
                    act.wait_ge(k_made, b * CHUNKS)
                nc.scalar.activation(hT_hi[:, k, :], proj_ps[:, k % 2, :], ACT.Relu).then_inc(hT_hi_done, 1)

            def parts_free(b, c):
                if not (isinstance(b, int) and b == 0 and c == 0):
                    act.wait_ge(stack_in, b * (CHUNKS * STACK_DMAS * 16) + c * STACK_DMAS * 16)

            def round_q(b, c):
                act.wait_ge(q_made, b * CHUNKS + (c + 1))
                parts_free(b, c)
                nc.scalar.activation(q_hi, proj_ps[:, 0, :], ACT.Copy, scale=HALF_SCALE).then_inc(q_hi_done, 1)

            def round_k(b, c):
                act.wait_ge(k_made, b * CHUNKS + (c + 1))
                parts_free(b, c)
                nc.scalar.activation(k_hi, proj_ps[:, 1, :], ACT.Copy).then_inc(k_hi_done, 1)

            def copy_v(b, nt):
                act.wait_ge(v_made, b * NT + (nt + 1))
                if nt == 0 and not (isinstance(b, int) and b == 0):
                    act.wait_ge(pv, b * PAIRS - 2)
                    act.wait_ge(v_moved, b)
                    if not (isinstance(b, int) and b == 1):
                        act.wait_ge(stored[NT - 1], b * 16 - 16)
                cut = (CHUNKS - 1) * P
                nc.scalar.activation(v_sb[:, nt, 0:cut], proj_ps[:, nt % 2, 0:cut], ACT.Copy).then_inc(v_copied, 1)
                nc.scalar.activation(v_side[:, nt, :], proj_ps[:, nt % 2, cut:D], ACT.Copy).then_inc(v_copied, 1)

            def copy_r(b, c):
                act.wait_ge(r_T, b * CHUNKS + (c + 1))
                if not (isinstance(b, int) and b == 0 and c == 0):
                    act.wait_ge(oT_lo_done, b * CHUNKS + c)
                nc.scalar.activation(oT[:, :], r_ps[:, :], ACT.Copy).then_inc(r_copied, 1)

            def round_o(b, c):
                act.wait_ge(oT_done, b * CHUNKS + (c + 1))
                if c == 0 and not (isinstance(b, int) and b == 0):
                    act.wait_ge(o_made, b * NT)
                nc.scalar.activation(oT_hi[:, c, :], oT[:, :], ACT.Copy).then_inc(oT_hi_done, 1)

            def body(b, first=False, last=False, drain=False):
                for u in range(UNITS if not drain else CU):
                    t = u % CU
                    if not drain:
                        exponentials(b, u)
                    if u in ACT_COPY_SLOTS and not (first and u < LAG) and not (drain and u >= LAG):
                        copy_pT(b, u - LAG)
                    if t == 4 and not (first and u < CU):
                        copy_r(b if u > CU else b - 1, (u // CU - 1) % CHUNKS)
                    if u in ROUND_O_PLAN and not (first and u < CU):
                        round_o(b if u > CU else b - 1, (u // CU - 1) % CHUNKS)
                    for (c, which), (_, rounded, _) in QK_PLAN.items():
                        if u == rounded and not drain and not (last and c == 0):
                            (round_q if which == "q" else round_k)(b if c else b + 1, c)
                    if u == 0 and not first and not drain:
                        copy_v(b, NT - 1)
                    if not last and not drain:
                        for nt in range(NT):
                            if u == NORMALISE_PLAN[nt]:
                                normalise(b + 1, nt)
                        if HT_SLOT <= u < HT_SLOT + KT:
                            round_hT(b + 1, u - HT_SLOT)
                        for nt in range(NT - 1):
                            if u == V_COPY_PLAN[nt]:
                                copy_v(b + 1, nt)

            for nt in range(NT):
                normalise(0, nt)
            round_w(1)
            for k in range(KT):
                round_hT(0, k)
            round_w(2)
            round_q(0, 0)
            round_k(0, 0)
            round_w(3)
            for nt in range(NT):
                copy_v(0, nt)
            samples(act, body)

        @block.gpsimd
        def _(pool):
            nc.gpsimd.memset(ident[:, :], 0.0).then_inc(ident_ready, 1)
            nc.gpsimd.memset(consts[:, 0, :], EPS).then_inc(consts_ready, 1)
            nc.gpsimd.memset(consts[:, 1, :], -0.5).then_inc(consts_ready, 1)
            nc.gpsimd.memset(consts[:, 2, :], -1.0).then_inc(consts_ready, 1)
            pool.wait_ge(ident_ready, 1)
            nc.gpsimd.affine_select(out=ident[:, :], in_=ident[:, :], compare_op=ALU.not_equal, fill=1.0, base=0,
                                    pattern=[[-1, P]], channel_multiplier=1).then_inc(ident_ready, 1)

            def inverse_deviation(b):
                pool.wait_ge(aggr_done, b * NT + NT)
                nc.gpsimd.tensor_tensor(var_eps[:, :], mean_var[:, :, 1], consts[:, 0, :], ALU.add).then_inc(rstd_done, 1)
                pool.wait_ge(rstd_done, b * 4 + 1)
                nc.gpsimd.tensor_tensor(rstd[:, :], var_eps[:, :], consts[:, 1, :], ALU.pow).then_inc(rstd_done, 1)
                pool.wait_ge(rstd_done, b * 4 + 2)
                nc.gpsimd.tensor_tensor(var_eps[:, :], rstd[:, :], consts[:, 2, :], ALU.mult).then_inc(rstd_done, 1)
                pool.wait_ge(rstd_done, b * 4 + 3)
                nc.gpsimd.tensor_tensor(shift[:, :], mean_var[:, :, 0], var_eps[:, :], ALU.mult).then_inc(rstd_done, 1)

            def repeat_r(b, c):
                pool.wait_ge(r_step, b * (4 * CHUNKS) + 4 * (c + 1))
                if not (isinstance(b, int) and b == 0 and c == 0):
                    pool.wait_ge(r_T, b * CHUNKS + c)
                nc.gpsimd.tensor_tensor(r_row[:, :, :], r_small[:, 0, :].unsqueeze(2).to_broadcast([P, CU, HD]),
                                        r_small[:, 3, :].unsqueeze(2).to_broadcast([P, CU, HD]),
                                        ALU.mult).then_inc(r_done, 1)

            def split_o(b, c):
                pool.wait_ge(oT_hi_done, b * CHUNKS + (c + 1))
                nc.gpsimd.tensor_tensor(oT_lo[:, c, :], oT[:, :], f(oT_hi[:, c, :]), ALU.subtract).then_inc(oT_lo_done, 1)

            def body(b, first=False, last=False, drain=False):
                for c in range(CHUNKS if not drain else 1):
                    if c == 2 and not last and not drain:
                        inverse_deviation(b + 1)
                    if not (first and c == 0):
                        repeat_r(b if c else b - 1, (c - 1) % CHUNKS)
                    if not (first and c == 0):
                        split_o(b if c else b - 1, (c - 1) % CHUNKS)

            pool.wait_ge(consts_ready, 3)
            inverse_deviation(0)
            pool.wait_ge(w_hi_done["o"], 1)
            nc.gpsimd.tensor_tensor(w_lo["o"][:, :, :], stage[:, 3], f(w_hi["o"][:, :, :]),
                                    ALU.subtract).then_inc(w_lo_done["o"], 1)
            samples(pool, body)


_INS = ["x", "adj", "wq_t", "wk_t", "wv_t", "wo_t"]


def kernel(x, adj, L0_gnn_Wq, L0_gnn_Wk, L0_gnn_Wv, L0_gnn_Wo):
    import numpy as np
    import concourse.bacc as bacc
    from concourse import mybir as mb
    from concourse.bass_utils import run_bass_kernel_spmd

    given = dict(zip(_INS, (x, adj, *(np.asarray(w).T for w in (L0_gnn_Wq, L0_gnn_Wk, L0_gnn_Wv, L0_gnn_Wo)))))
    nc = bacc.Bacc("TRN2", target_bir_lowering=False, num_devices=1)
    arrays, args = {}, []
    for name in _INS:
        a = np.ascontiguousarray(given[name])
        arrays[f"in_{name}"] = a
        args.append(nc.dram_tensor(f"in_{name}", a.shape, mb.dt.from_np(a.dtype), kind="ExternalInput").ap())
    shape = tuple(np.asarray(x).shape)
    args.append(nc.dram_tensor("out_0", shape, mb.dt.from_np(np.dtype("float32")), kind="ExternalOutput").ap())
    graph_attention(nc, *args)
    r = run_bass_kernel_spmd(nc, [arrays], core_ids=[0])
    return r.results[0]["out_0"]
```
